# Optimizing a Trainium2 kernel written in Bass

```python
import numpy as np
import jax
import jax.numpy as jnp

def _softmax(x, axis=-1):
    return jax.nn.softmax(x, axis=axis)

def _gelu(x):
    return jax.nn.gelu(x, approximate=True)

def _silu(x):
    return jax.nn.silu(x)

def _sigmoid(x):
    return jax.nn.sigmoid(x)

def _layernorm(x, axis=-1, eps=1e-05):
    m = jnp.mean(x, axis=axis, keepdims=True)
    v = jnp.var(x, axis=axis, keepdims=True)
    return (x - m) / jnp.sqrt(v + eps)

def _scatter_add(tgt, idx, src, axis=0):
    return tgt.at[idx].add(src)

def _segment_sum(src, seg, n):
    return jax.ops.segment_sum(src, seg, n)
kernel_name = 'mk_flamingo_gated_d1_seqx_r4_f06d11'

def setup_inputs(seed: int=0):
    np.random.seed(seed)
    _w = jnp.asarray

    def _rec_inputs():
        import jax
        import jax.numpy as jnp
        _rk = jax.random.key(seed)
        x = -0.0003929 + 0.9999 * jax.random.normal(jax.random.fold_in(_rk, 1), (128, 128, 256), jnp.float32)
        _lenS = 128 - jax.random.randint(jax.random.fold_in(_rk, 7), (128,), 0, max(1, 128 // 4) + 1, jnp.int32)
        _lenS2 = 128 - jax.random.randint(jax.random.fold_in(_rk, 8), (128,), 0, max(1, 128 // 4) + 1, jnp.int32)
        _ctx_768P = jax.random.normal(jax.random.fold_in(_rk, 11), (128, 16, 192), jnp.float32)
        _ctx_768c = jax.random.dirichlet(jax.random.fold_in(_rk, 511), 0.3 * jnp.ones((16,), jnp.float32), (128, 128))
        _ctx_768t = jnp.einsum('bsk,bkd->bsd', _ctx_768c, _ctx_768P)
        _ctx_768t = _ctx_768t * jax.lax.rsqrt(jnp.mean(jnp.square(_ctx_768t)) + 1e-12) * 0.953939
        ctx_768 = 0.00095986 + 0.999812 * (_ctx_768t + 0.3 * jax.random.normal(jax.random.fold_in(_rk, 611), (128, 128, 192), jnp.float32))
        _validS = jnp.arange(128)[None, :] < _lenS[:, None]
        _validS2 = jnp.arange(128)[None, :] < _lenS2[:, None]
        _causal = jnp.tril(jnp.ones((128, 128), dtype=bool))
        mask_BxS2_bf1 = jnp.ones((128, 128), dtype=bool)
        _g = jax.random.normal(jax.random.fold_in(_rk, 9001), (2, 1), jnp.float32)
        _g = jnp.sign(_g) * jnp.maximum(jnp.abs(_g), 1.0) + (_g == 0) * 1.0
        g_xattn = _g[0]
        g_ffn = _g[1]
        return (x, ctx_768, mask_BxS2_bf1, g_xattn, g_ffn)
    x, ctx_768, mask_BxS2_bf1, g_xattn, g_ffn = _rec_inputs()

    def _L0_xattn_setup():
        import jax, jax.numpy as jnp
        import numpy as np
        DIM = 256
        CTX_DIM = 192
        HEADS = 16
        key = jax.random.key(seed)
        ks = jax.random.split(key, 7)
        B, N, M = (4, 1024, 64)
        x = jax.random.normal(ks[0], (B, N, DIM), dtype=jnp.float32)
        context = jax.random.normal(ks[1], (B, M, CTX_DIM), dtype=jnp.float32)
        context_mask = jnp.ones((B, M), dtype=bool)
        s_d = 1.0 / np.sqrt(DIM)
        s_c = 1.0 / np.sqrt(CTX_DIM)
        Wq = jax.random.normal(ks[2], (DIM, DIM), dtype=jnp.float32) * s_d
        Wk = jax.random.normal(ks[3], (CTX_DIM, DIM), dtype=jnp.float32) * s_c
        Wv = jax.random.normal(ks[4], (CTX_DIM, DIM), dtype=jnp.float32) * s_c
        Wo = jax.random.normal(ks[5], (DIM, DIM), dtype=jnp.float32) * s_d
        return {'x': x, 'context': context, 'context_mask': context_mask, 'Wq': Wq, 'Wk': Wk, 'Wv': Wv, 'Wo': Wo}
    _L0_xattn_all = _L0_xattn_setup()
    _L0_xattn_in = {k: v for k, v in _L0_xattn_all.items() if k in ('Wq', 'Wk', 'Wv', 'Wo')}
    del _L0_xattn_all

    def _L0_ffn_setup():
        import jax, jax.numpy as jnp
        import numpy as np
        EMB = 256
        FF = 4 * EMB

        def _ternary(w):
            scale = jnp.maximum(jnp.mean(jnp.abs(w)), 1e-08)
            w_t = jnp.clip(jnp.round(w / scale), -1.0, 1.0)
            return w + jax.lax.stop_gradient(w_t - w)
        key = jax.random.key(seed)
        kx, k1, k2, kb1, kb2 = jax.random.split(key, 5)
        x = jax.random.normal(kx, (4, 512, EMB), dtype=jnp.float32)
        lim1 = 1.0 / np.sqrt(EMB)
        lim2 = 1.0 / np.sqrt(FF)
        W1 = jax.random.uniform(k1, (FF, EMB), jnp.float32, -lim1, lim1)
        b1 = jax.random.uniform(kb1, (FF,), jnp.float32, -lim1, lim1)
        W2 = jax.random.uniform(k2, (EMB, FF), jnp.float32, -lim2, lim2)
        b2 = jax.random.uniform(kb2, (EMB,), jnp.float32, -lim2, lim2)
        return {'x': x, 'W1': W1, 'b1': b1, 'W2': W2, 'b2': b2}
    _L0_ffn_all = _L0_ffn_setup()
    _L0_ffn_in = {k: v for k, v in _L0_ffn_all.items() if k in ('W1', 'b1', 'W2', 'b2')}
    del _L0_ffn_all
    return {'x': x, 'ctx_768': ctx_768, 'mask_BxS2_bf1': mask_BxS2_bf1, 'g_xattn': g_xattn, 'g_ffn': g_ffn, 'L0_xattn_Wq': _L0_xattn_in['Wq'], 'L0_xattn_Wk': _L0_xattn_in['Wk'], 'L0_xattn_Wv': _L0_xattn_in['Wv'], 'L0_xattn_Wo': _L0_xattn_in['Wo'], 'L0_ffn_W1': _L0_ffn_in['W1'], 'L0_ffn_b1': _L0_ffn_in['b1'], 'L0_ffn_W2': _L0_ffn_in['W2'], 'L0_ffn_b2': _L0_ffn_in['b2']}

def reference(x, ctx_768, mask_BxS2_bf1, g_xattn, g_ffn, L0_xattn_Wq, L0_xattn_Wk, L0_xattn_Wv, L0_xattn_Wo, L0_ffn_W1, L0_ffn_b1, L0_ffn_W2, L0_ffn_b2):
    import jax
    import jax.numpy as jnp

    def _L0_xattn_ref(x, context, context_mask, Wq, Wk, Wv, Wo):
        import jax, jax.numpy as jnp
        import numpy as np
        DIM = 256
        CTX_DIM = 192
        HEADS = 16
        B, N, _ = x.shape
        M = context.shape[1]
        hd = DIM // HEADS
        scale = hd ** (-0.5)
        q = (x @ Wq).reshape(B, N, HEADS, hd).transpose(0, 2, 1, 3)
        k = (context @ Wk).reshape(B, M, HEADS, hd).transpose(0, 2, 1, 3)
        v = (context @ Wv).reshape(B, M, HEADS, hd).transpose(0, 2, 1, 3)
        scores = jnp.einsum('bhid,bhjd->bhij', q, k) * scale
        max_neg = -jnp.finfo(scores.dtype).max
        scores = jnp.where(context_mask[:, None, None, :], scores, max_neg)
        attn = jax.nn.softmax(scores, axis=-1)
        out = jnp.einsum('bhij,bhjd->bhid', attn, v)
        out = out.transpose(0, 2, 1, 3).reshape(B, N, DIM)
        return out @ Wo

    def _L0_ffn_ref(x, W1, b1, W2, b2):
        import jax, jax.numpy as jnp
        import numpy as np
        EMB = 256
        FF = 4 * EMB

        def _ternary(w):
            scale = jnp.maximum(jnp.mean(jnp.abs(w)), 1e-08)
            w_t = jnp.clip(jnp.round(w / scale), -1.0, 1.0)
            return w + jax.lax.stop_gradient(w_t - w)
        h = jnp.einsum('bsd,fd->bsf', x, _ternary(W1)) + b1
        h = jax.nn.gelu(h, approximate=False)
        out = jnp.einsum('bsf,df->bsd', h, _ternary(W2)) + b2
        return out
    x = x + jnp.tanh(g_xattn[0]) * _L0_xattn_ref(_layernorm(x, axis=-1), ctx_768, mask_BxS2_bf1, L0_xattn_Wq, L0_xattn_Wk, L0_xattn_Wv, L0_xattn_Wo)
    x = x + jnp.tanh(g_ffn[0]) * _L0_ffn_ref(_layernorm(x, axis=-1), L0_ffn_W1, L0_ffn_b1, L0_ffn_W2, L0_ffn_b2)
    return x

_drawn_inputs = setup_inputs


def setup_inputs(seed=0):
    import zlib

    import numpy as np

    out = dict(_drawn_inputs(seed))
    spreads = {}
    factors = {'L0_ffn_b1': 22.894, 'L0_ffn_b2': 64.0}
    for name, (base, spread) in spreads.items():
        noise = np.random.default_rng([zlib.crc32(name.encode()), seed]).standard_normal(out[name].shape)
        drawn = base * np.exp(spread * noise) if base else spread * noise
        out[name] = jnp.asarray(drawn.astype(out[name].dtype))
    for name, factor in factors.items():
        out[name] = (out[name] * factor).astype(out[name].dtype)
    return out
```

```python
from contextlib import ExitStack

import concourse.bass as bass
from concourse import mybir

F32 = mybir.dt.float32
F16 = mybir.dt.float16
BF16 = mybir.dt.bfloat16
I32 = mybir.dt.int32
U8 = mybir.dt.uint8
ACT = mybir.ActivationFunctionType
ALU = mybir.AluOpType
AX = mybir.AxisListType

HEADS = 16
EPS = 1e-5
LN_PARTS = 4
NEWTON = 3
RSQRT_SEED = float(0x5F3759DF)
LN_STEPS = 4 + 3 * NEWTON


class Group:

    def __init__(self, half, parity):
        self.half, self.parity = half, parity

    def after(self, k):
        s = self.parity + k
        return Group(self.half + s // 2, s % 2)

    @property
    def n(self):
        return self.half * 2 + self.parity

    def batch(self, b):
        return self.half * 4 + (2 * self.parity + b)


def bass_gated_cross_attention_ternary_ffn(
    nc: bass.Bass, x, ctx_in, mask, g_xattn, g_ffn, wq, wk, wv, wo, w1, b1, w2, b2, out
):
    B, S, D = x.shape
    C = ctx_in.shape[2]
    FF = w1.shape[0]
    P = 128
    HD = D // HEADS
    KD = D // P
    C1 = C - P
    T = 2 * S
    NG = B // 2
    HB = P // HD
    UH = 4
    UNITS = HEADS // UH
    VC = 2 * HD + 1
    FB = FF // P
    QB = 4
    NQ = B // QB
    SCALE = float(HD) ** -0.5
    LAG = 2
    HBUF = 4
    assert S == P and D == KD * P and 0 < C1 <= P and UH * S == 512 and B % 8 == 0 and FB % HBUF == 0

    x_v = x.rearrange("b s d -> s b d")
    out_v = out.rearrange("b s d -> s b d")
    ctx_v = ctx_in.rearrange("b s c -> s b c")

    with ExitStack() as top:
        def sem(name):
            return top.enter_context(nc.semaphore(name))

        def sb(name, shape, dt, where=top):
            return where.enter_context(nc.sbuf_tensor(name, shape, dt))

        xres = sb("xres", [P, B, D], F32)
        ident = sb("ident", [P, P], F32)
        ident16 = sb("ident16", [P, P], BF16)
        ones = sb("ones", [P, P], F32)
        gates = sb("gates", [P, 4], F32)
        stats = sb("stats", [P, QB, 6], F32)
        meanvar = sb("meanvar", [P, QB, 2], F32)
        rstd = sb("rstd", [P, 3, QB], F32)
        gate_x, gate_f = gates[:, 2:3], gates[:, 3:4]

        one = ExitStack()
        wq_sb = sb("wq_sb", [P, KD, D], F32, one)
        wk_sb = sb("wk_sb", [P, 2, D], F32, one)
        wv_sb = sb("wv_sb", [P, 2, D], F32, one)
        wo_sb = sb("wo_sb", [P, KD, D], F32, one)
        minus = sb("minus", [P, HEADS, P], BF16, one)
        maskT = sb("maskT", [P, B], F32, one)
        vmask = sb("vmask", [P, B], F32, one)
        escale = sb("escale", [P, B], F32, one)
        masks = [sb(f"masks{p}", [P, 4], F32, one) for p in range(2)]
        ctx_sb = [sb(f"ctx_sb{p}", [P, 2, C], F32, one) for p in range(2)]
        xln = sb("xln", [P, 2, D], F32, one)
        xlnT = sb("xlnT", [P, KD, T], F32, one)
        ctxT = sb("ctxT", [P, 2, T], F32, one)
        q16 = [sb(f"q16_{p}", [P, 2, KD, T], F16, one) for p in range(2)]
        k16 = [sb(f"k16_{p}", [P, 2, KD, T], F16, one) for p in range(2)]
        qdiag = [sb(f"qdiag{p}", [P, 2, KD, HB, T], F16, one) for p in range(2)]
        v16 = [sb(f"v16_{p}", [P, 2, HEADS, VC], F16, one) for p in range(2)]
        prob = [sb(f"prob{p}", [P, UH * S], F32, one) for p in range(2)]
        probl = [sb(f"probl{p}", [P, UH * S], F16, one) for p in range(2)]
        smax = sb("smax", [P, 2, HEADS], F32, one)
        smax16 = sb("smax16", [P, 2, 2 * HEADS], BF16, one)
        smaxT = [sb(f"smaxT{p}", [P, S], BF16, one) for p in range(2)]
        rsum = sb("rsum", [P, 2, HEADS], F32, one)
        attn = [sb(f"attn{p}", [P, HEADS, HD], F32, one) for p in range(2)]
        attnT = sb("attnT", [P, KD, S], F32, one)
        one.close()

        two = ExitStack()
        w1T = sb("w1T", [P, KD, FF], BF16, two)
        w2T = sb("w2T", [P, FB, D], BF16, two)
        w1_raw = sb("w1_raw", [P, FB, D], F32, two)
        w2_raw = sb("w2_raw", [P, KD, FF], F32, two)
        w_neg = sb("w_neg", [P, FB * D], BF16, two)
        w1_t = sb("w1_t", [P, FB, D], BF16, two)
        w2_t = sb("w2_t", [P, KD, FF], BF16, two)
        wstat = sb("wstat", [P, 8], F32, two)
        b1_sb = sb("b1_sb", [P, FB], F32, two)
        b2_sb = sb("b2_sb", [P, D], F32, two)
        b2g = sb("b2g", [P, D], F32, two)
        yln = sb("yln", [P, QB, D], F32, two)
        y16 = [sb(f"y16_{p}", [P, 2, KD, QB * S], F16, two) for p in range(2)]
        hid = [sb(f"hid{p}", [P, QB * S], F32, two) for p in range(HBUF)]
        hidl = [sb(f"hidl{p}", [P, QB * S], F16, two) for p in range(HBUF)]
        ystage = [sb(f"ystage{p}", [P, QB, D], F32, two) for p in range(2)]
        two.close()

        bank = [top.enter_context(nc.psum_tensor(f"bank{i}", [P, 512], F32)) for i in range(8)]
        tr_bank, pj_bank = bank[0], bank[1]
        sm_bank, st_bank, pv_bank = bank[2:4], bank[4:6], bank[6:8]
        yt_bank, h_bank = bank[0:2], bank[2:4]
        y_bank = [bank[4:6], bank[6:8]]

        consts_set = sem("consts_set")
        weights_in = sem("weights_in")
        patterns_set = sem("patterns_set")
        mask_in = sem("mask_in")
        mask_f32 = sem("mask_f32")
        mask_transposed = sem("mask_transposed")
        mask_copied = sem("mask_copied")
        mask_counted = sem("mask_counted")
        mask_set = sem("mask_set")
        masks_picked = sem("masks_picked")
        gates_in = sem("gates_in")
        gates_set = sem("gates_set")
        x_in = [sem(f"x_in{p}") for p in range(2)]
        ctx_loaded = [sem(f"ctx_loaded{p}") for p in range(2)]
        ln_step = sem("ln_step")
        ln_done = sem("ln_done")
        x_transposed, xT_copied = sem("x_transposed"), sem("xT_copied")
        ctx_transposed, ctxT_copied = sem("ctx_transposed"), sem("ctxT_copied")
        q_made, q_high, q_split = sem("q_made"), sem("q_high"), sem("q_split")
        k_made, k_high, k_split = sem("k_made"), sem("k_high"), sem("k_split")
        v_made, v_high, v_split = sem("v_made"), sem("v_high"), sem("v_split")
        qdiag_in = [[sem(f"qdiag_in{p}_{m}") for m in range(KD)] for p in range(2)]
        rough_scored, max_taken = sem("rough_scored"), sem("max_taken")
        max_rounded, max_split = sem("max_rounded"), sem("max_split")
        max_transposed, maxT_copied = sem("max_transposed"), sem("maxT_copied")
        scored, exp_done, prob_split = sem("scored"), sem("exp_done"), sem("prob_split")
        weighed, sums_inverted, norm_read, norm_done = (
            sem("weighed"), sem("sums_inverted"), sem("norm_read"), sem("norm_done"))
        attn_transposed, attnT_copied = sem("attn_transposed"), sem("attnT_copied")
        projected, x1_done = sem("projected"), sem("x1_done")

        ffn_in, ffn_b2_in = sem("ffn_in"), sem("ffn_b2_in")
        w_step, w_summed, w_ternary = sem("w_step"), sem("w_summed"), sem("w_ternary")
        w_transposed, wT_copied = sem("w_transposed"), sem("wT_copied")
        b2_scaled = sem("b2_scaled")
        y_step, y_done = sem("y_step"), sem("y_done")
        y_transposed, y_high, y_split = sem("y_transposed"), sem("y_high"), sem("y_split")
        biased = sem("biased")
        h_made, gelu_done, h_split = sem("h_made"), sem("gelu_done"), sem("h_split")
        h_used, y_made, y_added = sem("h_used"), sem("y_made"), sem("y_added")
        y_out = [sem(f"y_out{p}") for p in range(2)]

        NC_SETS = 8
        def spread_queries(sp, g):
            sp.wait_ge(q_split, g.n + 1)
            for m in range(KD):
                for h in range(HB):
                    rows = slice(h * HD, (h + 1) * HD)
                    sp.dma_start(qdiag[g.parity][rows, :, m, h, :], q16[g.parity][rows, :, m, :]).then_inc(
                        qdiag_in[g.parity][m], 16)

        def load_x(sp, g):
            sp.dma_start(xres[:, bass.ds(g.batch(0), 2), :], x_v[:, bass.ds(g.batch(0), 2), :]).then_inc(
                x_in[g.parity], 16)

        def load_ctx(sp, g):
            sp.dma_start(ctx_sb[g.parity][:], ctx_v[:, bass.ds(g.batch(0), 2), :]).then_inc(
                ctx_loaded[g.parity], 16)

        def sp_group(sp, g, left):
            if left >= 3:
                sp.wait_ge(ln_done, 2 * (g.n + 2))
                load_x(sp, g.after(3))
            if left >= 3:
                sp.wait_ge(ctx_transposed, g.n + 2)
                load_ctx(sp, g.after(3))
            if left >= 1 and not (isinstance(g.half, int) and g.n == 0):
                sp.wait_ge(scored, 2 * UNITS * g.n)
                spread_queries(sp, g.after(1))
            elif left >= 1:
                spread_queries(sp, g.after(1))

        def transpose_x(pe, g, tr_free):
            pe.wait_ge(*tr_free)
            pe.wait_ge(ln_done, 2 * (g.n + 1))
            for k in range(KD):
                for b in range(2):
                    last = pe.transpose(tr_bank[:, k * T + b * S:k * T + (b + 1) * S],
                                        xln[:, b, k * P:(k + 1) * P], ident[:])
            last.then_inc(x_transposed, 1)
            return xT_copied, g.n + 1

        def transpose_ctx(pe, g, tr_free):
            if tr_free:
                pe.wait_ge(*tr_free)
            pe.wait_ge(ctx_loaded[g.parity], 16 * (g.half + 1))
            for b in range(2):
                pe.transpose(tr_bank[:, b * S:(b + 1) * S], ctx_sb[g.parity][:, b, 0:P], ident[:])
            for b in range(2):
                last = pe.transpose(tr_bank[0:C1, T + b * S:T + (b + 1) * S],
                                    ctx_sb[g.parity][:, b, P:C], ident[:])
            last.then_inc(ctx_transposed, 1)
            return ctxT_copied, g.n + 1

        def project_q(pe, g, m):
            if m == 0:
                pe.wait_ge(xT_copied, g.n + 1)
            for k in range(KD):
                last = pe.matmul(pj_bank[:, m * T:(m + 1) * T], wq_sb[:, k, m * P:(m + 1) * P],
                                 xlnT[:, k, :], start=(k == 0), stop=(k == KD - 1))
            if m == KD - 1:
                last.then_inc(q_made, 1)

        def project_k(pe, g, pj_free):
            pe.wait_ge(*pj_free)
            pe.wait_ge(ctxT_copied, g.n + 1)
            for m in range(KD):
                for k, rows in enumerate((P, C1)):
                    last = pe.matmul(pj_bank[:, m * T:(m + 1) * T], wk_sb[0:rows, k, m * P:(m + 1) * P],
                                     ctxT[0:rows, k, :], start=(k == 0), stop=(k == 1))
            last.then_inc(k_made, 1)
            return k_split, g.n + 1

        def project_v(pe, g, b):
            for k, rows in enumerate((P, C1)):
                last = pe.matmul(pj_bank[:, b * D:(b + 1) * D], ctxT[0:rows, k, b * S:(b + 1) * S],
                                 wv_sb[0:rows, k, :], start=(k == 0), stop=(k == 1))
            if b == 1:
                last.then_inc(v_made, 1)
            return v_split, g.n + 1

        def rough_scores(pe, g, b, u):
            n = g.batch(b) * UNITS + u
            if not (isinstance(n, int) and n < 2):
                pe.wait_ge(max_taken, n - 1)
            m, h0 = u * UH // HB, u * UH % HB
            if b == 0 and h0 == 0:
                pe.wait_ge(qdiag_in[g.parity][m], 16 * HB * (g.half + 1))
            if b == 0 and u == 0:
                pe.wait_ge(k_split, g.n + 1)
            cols = slice(b * S, (b + 1) * S)
            for c in range(UH):
                last = pe.matmul(sm_bank[u % 2][:, c * S:(c + 1) * S],
                                 qdiag[g.parity][:, 0, m, h0 + c, cols], k16[g.parity][:, 0, m, cols],
                                 start=True, stop=True)
            last.then_inc(rough_scored, 1)

        def transpose_max(pe, g, b, tr_free):
            pe.wait_ge(*tr_free)
            n = g.batch(b)
            pe.wait_ge(max_split, n + 1)
            pe.transpose(tr_bank[0:2 * HEADS, 0:S // 2].bitcast(BF16), smax16[:, b, :],
                         ident16[:]).then_inc(max_transposed, 1)
            return maxT_copied, n + 1

        def scores(pe, g, b, u):
            n = g.batch(b) * UNITS + u
            if u == 0:
                pe.wait_ge(maxT_copied, g.batch(b) + 1)
            if not (isinstance(n, int) and n < 2):
                pe.wait_ge(exp_done, n - 1)
            m, h0 = u * UH // HB, u * UH % HB
            cols = slice(b * S, (b + 1) * S)
            for kp, qp in ((0, 0), (0, 1), (1, 0)):
                pe.matmul(st_bank[u % 2][:], k16[g.parity][:, kp, m, cols],
                          qdiag[g.parity][:, qp, m, h0:h0 + UH, cols], start=(kp + qp == 0), stop=False,
                          skip_group_check=True)
            for c in range(UH):
                last = pe.matmul(st_bank[u % 2][:, c * S:(c + 1) * S], minus[:, u * UH + c, :],
                                 smaxT[b][:], start=False, stop=(c == UH - 1), skip_group_check=True)
            last.then_inc(scored, 1)

        def weigh(pe, g, b, u):
            n = g.batch(b)
            half, c0 = u // 2, u % 2 * UH
            pe.wait_ge(prob_split, n * UNITS + (u + 1))
            if b == 0 and u == 0:
                pe.wait_ge(v_split, g.n + 1)
            if u % 2 == 0 and not (isinstance(n, int) and n == 0):
                pe.wait_ge(norm_read, n * 2 + (half - 1))
            for c in range(UH):
                o = pv_bank[half][:, (c0 + c) * VC:(c0 + c + 1) * VC]
                v = v16[g.parity][:, b, u * UH + c, :]
                high = prob[u % 2][:].bitcast(BF16)[:, 2 * c * S + 1:2 * (c + 1) * S:2]
                pe.matmul(o, high, v, start=True, stop=False)
                last = pe.matmul(o, probl[u % 2][:, c * S:(c + 1) * S], v, start=False, stop=True)
            last.then_inc(weighed, 1)

        def transpose_attn(pe, n, b, tr_free):
            pe.wait_ge(*tr_free)
            pe.wait_ge(norm_done, 2 * n + 2)
            for k in range(KD):
                last = pe.transpose(tr_bank[:, k * S:(k + 1) * S],
                                    attn[b][:].rearrange("p h d -> p (h d)")[:, k * P:(k + 1) * P], ident[:])
            last.then_inc(attn_transposed, 1)
            return attnT_copied, n + 1

        def project_out(pe, n, pj_free):
            pe.wait_ge(*pj_free)
            pe.wait_ge(attnT_copied, n + 1)
            for k in range(KD):
                last = pe.matmul(pj_bank[:, 0:D], attnT[:, k, :], wo_sb[:, k, :], start=(k == 0),
                                 stop=(k == KD - 1))
            last.then_inc(projected, 1)
            return x1_done, n + 1

        def pe_first(pe):
            pe.wait_ge(consts_set, NC_SETS)
            pe.wait_ge(mask_f32, 1)
            pe.transpose(st_bank[0][:, 0:B], maskT[:], ident[:]).then_inc(mask_transposed, 1)
            pe.wait_ge(mask_copied, 1)
            pe.matmul(st_bank[1][:, 0:B], ones[:], vmask[:], start=True, stop=True).then_inc(mask_counted, 1)
            g0, g1 = Group(0, 0), Group(0, 1)
            pe.wait_ge(ln_done, 2)
            tr = transpose_x(pe, g0, (ln_done, 2))
            pe.wait_ge(weights_in, 16 * 6)
            for m in range(KD):
                project_q(pe, g0, m)
            tr = transpose_ctx(pe, g0, tr)
            project_k(pe, g0, (q_split, 1))
            pe.wait_ge(k_split, 1)
            for b in range(2):
                project_v(pe, g0, b)
            tr = transpose_ctx(pe, g1, tr)
            tr = transpose_x(pe, g1, tr)
            pe.wait_ge(v_split, 1)
            for m in range(KD):
                project_q(pe, g1, m)
            for u in range(UNITS):
                rough_scores(pe, g0, 0, u)
            transpose_max(pe, g0, 0, tr)

        def pe_group(pe, g, left):
            first = isinstance(g.half, int) and g.n == 0
            g1, g2 = g.after(1), g.after(2)
            tr = (maxT_copied, g.batch(0) + 1)
            pj = (q_split, g.n + 2) if left >= 1 else (x1_done, g.batch(0) - 1)
            for u in range(UNITS):
                rough_scores(pe, g, 1, u)
                scores(pe, g, 0, u)
                if u:
                    weigh(pe, g, 0, u - 1)
                if u == 0 and left >= 1:
                    pj = project_k(pe, g1, pj)
                if u == 1 and not first:
                    tr = transpose_attn(pe, g.batch(0) - 1, 1, tr)
                if u == 2 and not first:
                    pj = project_out(pe, g.batch(0) - 1, pj)
            if left >= 1:
                pe.wait_ge(*pj)
                project_v(pe, g1, 0)
            tr = transpose_max(pe, g, 1, tr)
            if left >= 1:
                pj = project_v(pe, g1, 1)
            weigh(pe, g, 0, UNITS - 1)
            for u in range(UNITS):
                if left >= 1:
                    rough_scores(pe, g1, 0, u)
                scores(pe, g, 1, u)
                if u:
                    weigh(pe, g, 1, u - 1)
                if u == 0 and left >= 2:
                    tr = transpose_x(pe, g2, tr)
                if u == 1:
                    tr = transpose_attn(pe, g.batch(0), 0, tr)
                if u == 2:
                    pj = project_out(pe, g.batch(0), pj)
                if u == 3 and left >= 2:
                    tr = transpose_ctx(pe, g2, tr)
            if left >= 2:
                pe.wait_ge(*pj)
                project_q(pe, g2, 0)
            if left >= 1:
                transpose_max(pe, g1, 0, tr)
            if left >= 2:
                project_q(pe, g2, 1)
            weigh(pe, g, 1, UNITS - 1)
            if left == 0:
                tr = transpose_attn(pe, g.batch(1), 1, tr)
                project_out(pe, g.batch(1), pj)

        def copy_xT(act, g):
            act.wait_ge(x_transposed, g.n + 1)
            if not (isinstance(g.half, int) and g.n == 0):
                act.wait_ge(q_made, g.n)
            act.copy(xlnT[:].rearrange("p k t -> p (k t)"), tr_bank[:]).then_inc(xT_copied, 1)

        def copy_ctxT(act, g):
            act.wait_ge(ctx_transposed, g.n + 1)
            if not (isinstance(g.half, int) and g.n == 0):
                act.wait_ge(v_made, g.n)
            act.copy(ctxT[:, 0, :], tr_bank[:, 0:T])
            act.copy(ctxT[0:C1, 1, :], tr_bank[0:C1, T:2 * T]).then_inc(ctxT_copied, 1)

        def high_q(act, g):
            act.wait_ge(q_made, g.n + 1)
            if not (isinstance(g.half, int) and g.n < 2):
                act.wait_ge(qdiag_in[g.parity][KD - 1], 16 * HB * g.half)
                act.wait_ge(qdiag_in[g.parity][0], 16 * HB * g.half)
            act.copy(q16[g.parity][:, 0].rearrange("p k t -> p (k t)"), pj_bank[:]).then_inc(q_high, 1)

        def high_k(act, g):
            act.wait_ge(k_made, g.n + 1)
            if not (isinstance(g.half, int) and g.n < 2):
                act.wait_ge(scored, 2 * UNITS * (g.n - 1))
            act.copy(k16[g.parity][:, 0].rearrange("p k t -> p (k t)"), pj_bank[:]).then_inc(k_high, 1)

        def high_v(act, g):
            act.wait_ge(v_made, g.n + 1)
            if not (isinstance(g.half, int) and g.n < 2):
                act.wait_ge(weighed, 2 * UNITS * (g.n - 1))
            act.wait_ge(masks_picked, g.n + 1)
            for b in range(2):
                last = act.activation(v16[g.parity][:, b, :, 0:HD],
                                      pj_bank[:, b * D:(b + 1) * D].rearrange("p (h d) -> p h d", h=HEADS),
                                      ACT.Identity, bias=0.0, scale=masks[g.parity][:, b:b + 1])
            last.then_inc(v_high, 1)

        def copy_maxT(act, g, b):
            n = g.batch(b)
            act.wait_ge(max_transposed, n + 1)
            act.copy(smaxT[b][0:2 * HEADS, :],
                     tr_bank[0:2 * HEADS, 0:S // 2].bitcast(BF16)).then_inc(maxT_copied, 1)

        def exponentials(act, g, b, u):
            n = g.batch(b) * UNITS + u
            act.wait_ge(scored, n + 1)
            if not (isinstance(n, int) and n < 2):
                act.wait_ge(weighed, n - 1)
            act.activation(prob[u % 2][:], st_bank[u % 2][:], ACT.Exp, bias=0.0,
                           scale=masks[g.parity][:, 2 + b:3 + b]).then_inc(exp_done, 1)

        def copy_attnT(act, n):
            act.wait_ge(attn_transposed, n + 1)
            if not (isinstance(n, int) and n == 0):
                act.wait_ge(projected, n)
            act.copy(attnT[:].rearrange("p k t -> p (k t)"), tr_bank[:, 0:KD * S]).then_inc(attnT_copied, 1)

        def act_first(act):
            act.wait_ge(gates_in, 32)
            act.activation(gates[:, 2:4], gates[:, 0:2], ACT.Tanh).then_inc(gates_set, 1)
            g0, g1 = Group(0, 0), Group(0, 1)
            copy_xT(act, g0)
            high_q(act, g0)
            copy_ctxT(act, g0)
            high_k(act, g0)
            high_v(act, g0)
            copy_ctxT(act, g1)
            copy_xT(act, g1)
            copy_maxT(act, g0, 0)
            high_q(act, g1)

        def act_group(act, g, left):
            first = isinstance(g.half, int) and g.n == 0
            g1, g2 = g.after(1), g.after(2)
            for u in range(UNITS):
                if u == 1 and left >= 1:
                    high_k(act, g1)
                if u == 2 and not first:
                    copy_attnT(act, g.batch(0) - 1)
                exponentials(act, g, 0, u)
            copy_maxT(act, g, 1)
            if left >= 1:
                high_v(act, g1)
            for u in range(UNITS):
                if u == 1 and left >= 2:
                    copy_xT(act, g2)
                if u == 2:
                    copy_attnT(act, g.batch(0))
                exponentials(act, g, 1, u)
            if left >= 2:
                copy_ctxT(act, g2)
            if left >= 1:
                copy_maxT(act, g1, 0)
            if left >= 2:
                high_q(act, g2)
            if left == 0:
                copy_attnT(act, g.batch(1))

        def ln_statistics(dve, rows, step, base):
            n = len(rows)
            for i, r in enumerate(rows):
                last = dve.bn_stats(stats[:, i, :], r)
            last.then_inc(step, 1)
            dve.wait_ge(step, base + 1)
            dve.tensor_copy(rstd[:, 2, 0:n], stats[:, 0:n, 1])
            for i in range(n):
                last = dve.bn_aggr(meanvar[:, i, :], stats[:, i, :])
            last.then_inc(step, 1)

        def ln_seed(dve, n, step, base):
            half, y, t = rstd[:, 0, 0:n], rstd[:, 1, 0:n], rstd[:, 2, 0:n]
            dve.wait_ge(step, base + 2)
            dve.tensor_scalar(t, meanvar[:, 0:n, 1], EPS, None, ALU.add).then_inc(step, 1)
            dve.wait_ge(step, base + 3)
            dve.tensor_scalar(y.bitcast(I32), t.bitcast(I32), -0.5, RSQRT_SEED, ALU.mult,
                              ALU.add)
            dve.tensor_scalar(half, t, -0.5, None, ALU.mult).then_inc(step, 1)

        def ln_newton(dve, n, step, base, k):
            half, y, t = rstd[:, 0, 0:n], rstd[:, 1, 0:n], rstd[:, 2, 0:n]
            at = base + 4 + 3 * k
            dve.wait_ge(step, at)
            dve.tensor_tensor(t, y, y, ALU.mult).then_inc(step, 1)
            dve.wait_ge(step, at + 1)
            dve.tensor_tensor(t, t, half, ALU.mult).then_inc(step, 1)
            dve.wait_ge(step, at + 2)
            dve.scalar_tensor_tensor(y, t, 1.5, y, ALU.add, ALU.mult).then_inc(step, 1)

        def ln_apply(dve, rows, outs, step, base, done):
            dve.wait_ge(step, base + LN_STEPS)
            for i, (r, o) in enumerate(zip(rows, outs)):
                dve.tensor_scalar(o, r, meanvar[:, i, 0:1], rstd[:, 1, i:i + 1], ALU.subtract,
                                  ALU.mult).then_inc(done, 1)

        def x_rows(g):
            return [xres[:, bass.ds(g.batch(b), 1), :].rearrange("p o d -> p (o d)") for b in range(2)]

        def norm_x(dve, g, part):
            base = g.n * LN_STEPS
            if part == 0:
                dve.wait_ge(x_in[g.parity], 16 * (g.half + 1))
                ln_statistics(dve, x_rows(g), ln_step, base)
            if part == 1:
                ln_seed(dve, 2, ln_step, base)
                ln_newton(dve, 2, ln_step, base, 0)
            if part == 2:
                for k in range(1, NEWTON):
                    ln_newton(dve, 2, ln_step, base, k)
            if part == 3:
                if not (isinstance(g.half, int) and g.n == 0):
                    dve.wait_ge(x_transposed, g.n)
                ln_apply(dve, x_rows(g), [xln[:, b, :] for b in range(2)], ln_step, base, ln_done)

        def low_q(dve, g):
            dve.wait_ge(q_high, g.n + 1)
            dve.tensor_tensor(q16[g.parity][:, 1].rearrange("p k t -> p (k t)"), pj_bank[:],
                              q16[g.parity][:, 0].rearrange("p k t -> p (k t)"),
                              ALU.subtract).then_inc(q_split, 1)

        def low_k(dve, g):
            dve.wait_ge(k_high, g.n + 1)
            dve.tensor_tensor(k16[g.parity][:, 1].rearrange("p k t -> p (k t)"), pj_bank[:],
                              k16[g.parity][:, 0].rearrange("p k t -> p (k t)"),
                              ALU.subtract).then_inc(k_split, 1)

        def pick_masks(dve, g):
            if not (isinstance(g.half, int) and g.n < 2):
                dve.wait_ge(exp_done, 2 * UNITS * (g.n - 1))
            dve.tensor_scalar(masks[g.parity][:, 0:2], vmask[:, bass.ds(g.batch(0), 2)], 1.0, None, ALU.mult)
            dve.tensor_scalar(masks[g.parity][:, 2:4], escale[:, bass.ds(g.batch(0), 2)], 1.0, None,
                              ALU.mult).then_inc(masks_picked, 1)

        def low_v(dve, g):
            dve.wait_ge(v_high, g.n + 1)
            for b in range(2):
                dve.tensor_copy(v16[g.parity][:, b, :, 2 * HD:VC],
                                masks[g.parity][:, b:b + 1].unsqueeze(2).to_broadcast([P, HEADS, 1]))
                last = dve.scalar_tensor_tensor(
                    v16[g.parity][:, b, :, HD:2 * HD],
                    pj_bank[:, b * D:(b + 1) * D].rearrange("p (h d) -> p h d", h=HEADS),
                    masks[g.parity][:, b:b + 1], v16[g.parity][:, b, :, 0:HD], ALU.mult, ALU.subtract)
            last.then_inc(v_split, 1)

        def take_max(dve, g, b, u):
            n = g.batch(b) * UNITS + u
            dve.wait_ge(rough_scored, n + 1)
            dve.tensor_reduce(smax[:, b, u * UH:(u + 1) * UH],
                              sm_bank[u % 2][:].rearrange("p (h j) -> p h j", h=UH), AX.X,
                              ALU.max).then_inc(max_taken, 1)

        def split_max(dve, g, b):
            n = g.batch(b)
            dve.wait_ge(max_taken, (n + 1) * UNITS)
            dve.tensor_copy(smax16[:, b, 0:HEADS], smax[:, b, :]).then_inc(max_rounded, 1)
            dve.wait_ge(max_rounded, n + 1)
            dve.tensor_tensor(smax16[:, b, HEADS:2 * HEADS], smax[:, b, :], smax16[:, b, 0:HEADS],
                              ALU.subtract).then_inc(max_split, 1)

        def normalise(dve, n, b, half):
            hb = HEADS // 2
            heads = slice(half * hb, (half + 1) * hb)
            dve.wait_ge(weighed, n * UNITS + 2 * (half + 1))
            if not (isinstance(n, int) and n < 2):
                dve.wait_ge(attn_transposed, n - 1)
            pv = pv_bank[half][:, 0:hb * VC].rearrange("p (h c) -> p h c", h=hb)
            dve.reciprocal(rsum[:, b, heads], pv[:, :, 2 * HD])
            dve.tensor_reduce(attn[b][:, heads, :],
                              pv[:, :, 0:2 * HD].rearrange("p h (two d) -> p h d two", two=2), AX.X,
                              ALU.add).then_inc(norm_read, 1)
            dve.wait_ge(norm_read, n * 2 + (half + 1))
            dve.tensor_tensor(attn[b][:, heads, :], attn[b][:, heads, :],
                              rsum[:, b, heads].unsqueeze(2).to_broadcast([P, hb, HD]),
                              ALU.mult).then_inc(norm_done, 1)

        def add_attention(dve, n):
            dve.wait_ge(projected, n + 1)
            row = xres[:, bass.ds(n, 1), :].rearrange("p o d -> p (o d)")
            dve.scalar_tensor_tensor(row, pj_bank[:, 0:D], gate_x, row, ALU.mult, ALU.add).then_inc(x1_done, 1)

        def dve_first(dve):
            dve.memset(qdiag[0][:].rearrange("p a b c d -> p (a b c d)").bitcast(F32), 0.0).then_inc(consts_set, 1)
            for p in range(2):
                dve.memset(smaxT[p][:], 0.0).then_inc(consts_set, 1)
            dve.memset(ones[:], 1.0).then_inc(consts_set, 1)
            dve.wait_ge(mask_in, 16)
            dve.tensor_copy(maskT[:], escale[:].bitcast(U8)[:, 0:B]).then_inc(mask_f32, 1)
            g0, g1 = Group(0, 0), Group(0, 1)
            for part in range(LN_PARTS):
                norm_x(dve, g0, part)
            dve.wait_ge(mask_transposed, 1)
            dve.tensor_copy(vmask[:], st_bank[0][:, 0:B]).then_inc(mask_copied, 1)
            dve.wait_ge(mask_counted, 1)
            dve.tensor_scalar(maskT[:], st_bank[1][:, 0:B], 0.5, None, ALU.is_lt)
            dve.tensor_scalar(escale[:], st_bank[1][:, 0:B], 0.5, SCALE, ALU.is_gt, ALU.mult).then_inc(mask_f32, 1)
            dve.wait_ge(mask_f32, 2)
            dve.tensor_tensor(vmask[:], vmask[:], maskT[:], ALU.max).then_inc(mask_set, 1)
            dve.wait_ge(mask_set, 1)
            dve.wait_ge(gates_set, 1)
            pick_masks(dve, g0)
            for part in range(LN_PARTS):
                norm_x(dve, g1, part)
            low_q(dve, g0)
            low_k(dve, g0)
            low_v(dve, g0)
            for u in range(UNITS):
                take_max(dve, g0, 0, u)
            split_max(dve, g0, 0)

        def dve_group(dve, g, left):
            first = isinstance(g.half, int) and g.n == 0
            g1, g2 = g.after(1), g.after(2)
            if left >= 1:
                low_q(dve, g1)
                pick_masks(dve, g1)
            for u in range(UNITS):
                if u == 3 and not first:
                    add_attention(dve, g.batch(0) - 1)
                take_max(dve, g, 1, u)
                if u == 0 and not first:
                    normalise(dve, g.batch(0) - 1, 1, 1)
                if u == 1 and left >= 1:
                    low_k(dve, g1)
                if u < 3 and left >= 2:
                    norm_x(dve, g2, u)
            split_max(dve, g, 1)
            if left >= 2:
                norm_x(dve, g2, 3)
            normalise(dve, g.batch(0), 0, 0)
            if left >= 1:
                low_v(dve, g1)
            for u in range(UNITS):
                if u == 3:
                    add_attention(dve, g.batch(0))
                if left >= 1:
                    take_max(dve, g1, 0, u)
                if u == 0:
                    normalise(dve, g.batch(0), 0, 1)
            if left >= 1:
                split_max(dve, g1, 0)
            normalise(dve, g.batch(1), 1, 0)
            if left == 0:
                normalise(dve, g.batch(1), 1, 1)
                add_attention(dve, g.batch(1))

        def low_prob(pool, g, b, u):
            n = g.batch(b) * UNITS + u
            pool.wait_ge(exp_done, n + 1)
            pool.tensor_tensor(probl[u % 2][:], prob[u % 2][:], prob[u % 2][:].bitcast(BF16)[:, 1::2],
                               ALU.subtract).then_inc(prob_split, 1)

        def pool_group(pool, g, left):
            for b in range(2):
                for u in range(UNITS):
                    low_prob(pool, g, b, u)

        def over_pairs(engine, do, pairs, apart=1):
            for s in range(2):
                do(engine, Group(0, s), 2 * pairs - 1 - s)
            with engine.Fori(1, pairs - apart) as i:
                for s in range(2):
                    do(engine, Group(i, s), 2 * apart + 1 - s)
            for r in range(pairs - apart, pairs):
                for s in range(2):
                    do(engine, Group(r, s), 2 * (pairs - r) - 1 - s)

        def over_groups(engine, do, apart=1):
            over_pairs(engine, do, NG // 2, apart)

        def steps(engine, do):
            over_pairs(engine, do, NQ // 2)

        def prepare_weights_dve(dve):
            dve.wait_ge(ffn_in, 16 * 3)
            for i, raw in enumerate((w1_raw, w2_raw)):
                dve.tensor_reduce(wstat[:, i:i + 1], raw[:].rearrange("p a b -> p (a b)"), AX.X, ALU.add,
                                  apply_absolute_value=True).then_inc(w_step, 1)
            dve.wait_ge(w_summed, 1)
            half_mean = 0.5 / float(FF * D)
            dve.tensor_scalar(wstat[:, 2:4], h_bank[0][:, 0:2], half_mean, 0.5e-8, ALU.mult,
                              ALU.max).then_inc(w_step, 1)
            dve.wait_ge(w_step, 3)
            dve.tensor_scalar(wstat[:, 4:6], wstat[:, 2:4], -1.0, None, ALU.mult).then_inc(w_step, 1)
            dve.wait_ge(w_step, 4)
            for i, (raw, tern) in enumerate(((w1_raw, w1_t), (w2_raw, w2_t))):
                flat = raw[:].rearrange("p a b -> p (a b)")
                dve.tensor_scalar(w_neg[:], flat, wstat[:, 4 + i:5 + i], None, ALU.is_lt).then_inc(w_step, 1)
                dve.wait_ge(w_step, 5 + i)
                dve.scalar_tensor_tensor(tern[:].rearrange("p a b -> p (a b)"), flat, wstat[:, 2 + i:3 + i],
                                         w_neg[:], ALU.is_gt, ALU.subtract).then_inc(w_ternary, 1)
                dve.wait_ge(w_ternary, 1 + i)
            dve.wait_ge(ffn_b2_in, 16)
            dve.tensor_scalar(b2g[:], b2_sb[:], gate_f, None, ALU.mult).then_inc(b2_scaled, 1)

        def prepare_weights_pe(pe):
            pe.wait_ge(w_step, 2)
            pe.wait_ge(x1_done, B)
            pe.matmul(h_bank[0][:, 0:2], ones[:], wstat[:, 0:2], start=True, stop=True).then_inc(w_summed, 1)
            n = 0
            for i, (tern, rows, cols) in enumerate(((w1_t, FB, KD), (w2_t, KD, FB))):
                pe.wait_ge(w_ternary, i + 1)
                for c in range(cols):
                    for r in range(rows):
                        q, o = n // 8, n % 8
                        if o == 0 and q >= 2:
                            pe.wait_ge(wT_copied, q - 1)
                        last = pe.transpose(y_bank[0][q % 2][:].bitcast(BF16)[:, o * P:(o + 1) * P],
                                            tern[:, r, c * P:(c + 1) * P], ident16[:])
                        n += 1
                        if o == 7:
                            last.then_inc(w_transposed, 1)

        def prepare_weights_act(act):
            flat = [w1T[:, k, :] for k in range(KD)] + [
                w2T[:, 4 * q:4 * q + 4, :].rearrange("p f d -> p (f d)") for q in range(FB // 4)]
            for q, dst in enumerate(flat):
                act.wait_ge(w_transposed, q + 1)
                act.copy(dst, y_bank[0][q % 2][:].bitcast(BF16)).then_inc(wT_copied, 1)

        def norm_y(dve, g, part):
            base = g.n * LN_STEPS
            rows = [xres[:, bass.ds(g.n * QB + b, 1), :].rearrange("p o d -> p (o d)") for b in range(QB)]
            if part == 0:
                ln_statistics(dve, rows, y_step, base)
            if part == 1:
                ln_seed(dve, QB, y_step, base)
                ln_newton(dve, QB, y_step, base, 0)
            if part == 2:
                for k in range(1, NEWTON):
                    ln_newton(dve, QB, y_step, base, k)
            if part == 3:
                if not (isinstance(g.half, int) and g.n == 0):
                    dve.wait_ge(y_transposed, 2 * g.n)
                ln_apply(dve, rows, [yln[:, b, :] for b in range(QB)], y_step, base, y_done)

        def transpose_y(pe, g):
            pe.wait_ge(y_done, QB * (g.n + 1))
            for k in range(KD):
                if not (isinstance(g.half, int) and g.n == 0):
                    pe.wait_ge(y_split, KD * g.n)
                for b in range(QB):
                    last = pe.transpose(yt_bank[k][:, b * S:(b + 1) * S], yln[:, b, k * P:(k + 1) * P], ident[:])
                last.then_inc(y_transposed, 1)

        def high_y(act, g):
            for k in range(KD):
                act.wait_ge(y_transposed, KD * g.n + (k + 1))
                if k == 0 and not (isinstance(g.half, int) and g.n < 2):
                    act.wait_ge(h_made, FB * (g.n - 1))
                act.copy(y16[g.parity][:, 0, k, :], yt_bank[k][:]).then_inc(y_high, 1)

        def low_y(dve, g):
            for k in range(KD):
                dve.wait_ge(y_high, KD * g.n + (k + 1))
                dve.tensor_tensor(y16[g.parity][:, 1, k, :], yt_bank[k][:], y16[g.parity][:, 0, k, :],
                                  ALU.subtract).then_inc(y_split, 1)

        def hidden(pe, g, f):
            n = g.n * FB + f
            if f == 0:
                pe.wait_ge(y_split, KD * (g.n + 1))
            if not (isinstance(n, int) and n < 2):
                pe.wait_ge(gelu_done, n - 1)
            i = 0
            for k in range(KD):
                for part in range(2):
                    last = pe.matmul(h_bank[f % 2][:], w1T[:, k, f * P:(f + 1) * P], y16[g.parity][:, part, k, :],
                                     start=(i == 0), stop=(i == 2 * KD - 1))
                    i += 1
            last.then_inc(h_made, 1)

        def gelu(act, g, f):
            n = g.n * FB + f
            act.wait_ge(h_made, n + 1)
            if not (isinstance(n, int) and n < HBUF):
                act.wait_ge(h_used, n - (HBUF - 1))
            act.activation(hid[f % HBUF][:], h_bank[f % 2][:], ACT.Gelu, bias=b1_sb[:, f:f + 1]).then_inc(gelu_done, 1)

        def low_h(dve, g, f):
            n = g.n * FB + f
            dve.wait_ge(gelu_done, n + 1)
            dve.tensor_tensor(hidl[f % HBUF][:], hid[f % HBUF][:], hid[f % HBUF][:].bitcast(BF16)[:, 1::2],
                              ALU.subtract).then_inc(h_split, 1)

        def second(pe, g, f):
            n = g.n * FB + f
            if f == 0 and not (isinstance(g.half, int) and g.n < 2):
                pe.wait_ge(y_added, QB * (g.n - 1))
            pe.wait_ge(h_split, n + 1)
            for b in range(QB):
                o = y_bank[g.parity][b // 2][:, (b % 2) * D:(b % 2 + 1) * D]
                high = hid[f % HBUF][:].bitcast(BF16)[:, 2 * b * S + 1:2 * (b + 1) * S:2]
                pe.matmul(o, high, w2T[:, f, :], start=(f == 0 and b % 2 == 0), stop=False, skip_group_check=True)
                last = pe.matmul(o, hidl[f % HBUF][:, b * S:(b + 1) * S], w2T[:, f, :], start=False,
                                 stop=(f == FB - 1), skip_group_check=True)
            last.then_inc(h_used, 1)

        def pe_step(pe, g, left):
            first = isinstance(g.half, int) and g.n == 0
            for f in range(FB):
                hidden(pe, g, f)
                if f >= LAG:
                    second(pe, g, f - LAG)
                elif not first:
                    second(pe, Group(g.half - 1, 1) if g.parity == 0 else Group(g.half, 0), FB - LAG + f)
                if f == FB // 2 + 1 and left >= 1:
                    transpose_y(pe, g.after(1))
            if left == 0:
                for f in range(FB - LAG, FB):
                    second(pe, g, f)

        def act_step(act, g, left):
            for f in range(FB):
                gelu(act, g, f)
                if f == FB // 2 + 1 and left >= 1:
                    high_y(act, g.after(1))

        def add_y(dve, g):
            dve.wait_ge(h_used, FB * (g.n + 1))
            dve.wait_ge(biased, g.n + 1)
            if not (isinstance(g.half, int) and g.n < 2):
                dve.wait_ge(y_out[g.parity], 16 * g.half)
            for b in range(QB):
                o = y_bank[g.parity][b // 2][:, (b % 2) * D:(b % 2 + 1) * D]
                dve.scalar_tensor_tensor(ystage[g.parity][:, b, :], o, gate_f,
                                         xres[:, bass.ds(g.n * QB + b, 1), :].rearrange("p o d -> p (o d)"),
                                         ALU.mult, ALU.add).then_inc(y_added, 1)

        def dve_step(dve, g, left):
            first = isinstance(g.half, int) and g.n == 0
            for f in range(FB):
                low_h(dve, g, f)
                if f < LN_PARTS and left >= 1:
                    norm_y(dve, g.after(1), f)
                if f == LAG and not first:
                    add_y(dve, Group(g.half - 1, 1) if g.parity == 0 else Group(g.half, 0))
                if f == FB // 2 + 1 and left >= 1:
                    low_y(dve, g.after(1))
            if left == 0:
                add_y(dve, g)

        def pool_step(pool, g, left):
            pool.wait_ge(y_done, QB * (g.n + 1))
            rows = xres[:, bass.ds(g.n * QB, QB), :]
            pool.tensor_tensor(rows, rows, b2g[:].unsqueeze(1).to_broadcast([P, QB, D]), ALU.add).then_inc(biased, 1)

        def sp_step(sp, g, left):
            sp.wait_ge(y_added, QB * (g.n + 1))
            sp.dma_start(out_v[:, bass.ds(g.n * QB, QB), :], ystage[g.parity][:]).then_inc(y_out[g.parity], 16)

        block = top.enter_context(nc.Block())

        @block.sync
        def _(sp):
            sp.dma_start(escale[:].bitcast(U8)[:, 0:S], mask).then_inc(mask_in, 16)
            load_x(sp, Group(0, 0))
            load_ctx(sp, Group(0, 0))
            load_x(sp, Group(0, 1))
            sp.dma_start(wq_sb[:], wq.rearrange("(k p) n -> p k n", p=P)).then_inc(weights_in, 16)
            sp.dma_start(wk_sb[:, 0, :], wk[0:P, :]).then_inc(weights_in, 16)
            sp.dma_start(wk_sb[0:C1, 1, :], wk[P:C, :]).then_inc(weights_in, 16)
            sp.dma_start(wv_sb[:, 0, :], wv[0:P, :]).then_inc(weights_in, 16)
            sp.dma_start(wv_sb[0:C1, 1, :], wv[P:C, :]).then_inc(weights_in, 16)
            sp.dma_start(wo_sb[:], wo.rearrange("(k p) n -> p k n", p=P)).then_inc(weights_in, 16)
            load_ctx(sp, Group(0, 1))
            sp.dma_start(gates[:, 0:1], g_xattn.partition_broadcast(P)).then_inc(gates_in, 16)
            sp.dma_start(gates[:, 1:2], g_ffn.partition_broadcast(P)).then_inc(gates_in, 16)
            sp.wait_ge(ln_done, 2)
            load_x(sp, Group(1, 0))
            sp.wait_ge(ctx_transposed, 1)
            load_ctx(sp, Group(1, 0))
            sp.wait_ge(consts_set, NC_SETS)
            spread_queries(sp, Group(0, 0))
            over_groups(sp, sp_group, 2)
            sp.wait_ge(x1_done, B)
            sp.dma_start(w1_raw[:], w1.rearrange("(f p) d -> p f d", p=P)).then_inc(ffn_in, 16)
            sp.dma_start(w2_raw[:], w2.rearrange("(k p) f -> p k f", p=P)).then_inc(ffn_in, 16)
            with nc.allow_non_contiguous_dma(reason="1024 biases, one a row"):
                sp.dma_start(b1_sb[:], b1.rearrange("(f p) -> p f", p=P)).then_inc(ffn_in, 16)
            sp.dma_start(b2_sb[:], b2.partition_broadcast(P)).then_inc(ffn_b2_in, 16)
            steps(sp, sp_step)
            for p in range(2):
                sp.wait_ge(y_out[p], 16 * (NQ // 2))

        @block.gpsimd
        def _(pool):
            pool.memset(ident[:], 0.0).then_inc(consts_set, 1)
            pool.memset(minus[:], 0.0).then_inc(consts_set, 1)
            pool.memset(qdiag[1][:].rearrange("p a b c d -> p (a b c d)").bitcast(F32), 0.0).then_inc(consts_set, 1)
            pool.wait_ge(consts_set, 7)
            pool.affine_select(out=ident[:], in_=ident[:], compare_op=ALU.not_equal, fill=1.0, base=0,
                               pattern=[[-1, P]], channel_multiplier=1).then_inc(patterns_set, 1)
            for part in range(2):
                if part:
                    pool.wait_ge(patterns_set, 2)
                pool.affine_select(out=minus[:], in_=minus[:], compare_op=ALU.not_equal, fill=-1.0,
                                   base=-HEADS * part, pattern=[[-1, HEADS], [0, P]],
                                   channel_multiplier=1).then_inc(patterns_set, 1)
            pool.wait_ge(patterns_set, 3)
            pool.tensor_copy(ident16[:], ident[:]).then_inc(consts_set, 1)
            over_groups(pool, pool_group)
            pool.wait_ge(b2_scaled, 1)
            steps(pool, pool_step)

        @block.tensor
        def _(pe):
            pe_first(pe)
            over_groups(pe, pe_group)
            prepare_weights_pe(pe)
            transpose_y(pe, Group(0, 0))
            pe.wait_ge(wT_copied, 4)
            steps(pe, pe_step)

        @block.scalar
        def _(act):
            act_first(act)
            over_groups(act, act_group)
            prepare_weights_act(act)
            high_y(act, Group(0, 0))
            steps(act, act_step)

        @block.vector
        def _(dve):
            dve_first(dve)
            over_groups(dve, dve_group)
            dve.wait_ge(x1_done, B)
            prepare_weights_dve(dve)
            for part in range(LN_PARTS):
                norm_y(dve, Group(0, 0), part)
            low_y(dve, Group(0, 0))
            steps(dve, dve_step)


_INS = ["x", "ctx_768", "mask_BxS2_bf1", "g_xattn", "g_ffn", "L0_xattn_Wq", "L0_xattn_Wk", "L0_xattn_Wv",
        "L0_xattn_Wo", "L0_ffn_W1", "L0_ffn_b1", "L0_ffn_W2", "L0_ffn_b2"]
_OUTS = [((128, 128, 256), "float32")]


def kernel(**inputs):
    import numpy as _np
    import concourse.bacc as _bacc
    from concourse import mybir as _mybir
    from concourse.bass_utils import run_bass_kernel_spmd as _run

    nc = _bacc.Bacc("TRN2", target_bir_lowering=False, num_devices=1)
    arrays, args = {}, []
    for name in _INS:
        a = _np.ascontiguousarray(inputs[name])
        arrays[f"in_{name}_dram"] = a
        args.append(nc.dram_tensor(f"in_{name}_dram", a.shape, _mybir.dt.from_np(a.dtype), kind="ExternalInput").ap())
    for i, (shape, dtype) in enumerate(_OUTS):
        dt = _mybir.dt.from_np(_np.dtype(dtype))
        args.append(nc.dram_tensor(f"out_{i}_dram", shape, dt, kind="ExternalOutput").ap())
    bass_gated_cross_attention_ternary_ffn(nc, *args)
    r = _run(nc, [arrays], core_ids=[0])
    got = tuple(r.results[0][f"out_{i}_dram"] for i in range(len(_OUTS)))
    return got[0]
```

```python
from contextlib import ExitStack

import concourse.bass as bass
from concourse import mybir

F32 = mybir.dt.float32
F16 = mybir.dt.float16
BF16 = mybir.dt.bfloat16
I32 = mybir.dt.int32
U8 = mybir.dt.uint8
ACT = mybir.ActivationFunctionType
ALU = mybir.AluOpType
AX = mybir.AxisListType

HEADS = 16
EPS = 1e-5
NEWTON = 3
LN_B = 8
RSQRT_SEED = float(0x5F3759DF)
LN_PARTS = 5 + 3 * NEWTON


class Group:

    def __init__(self, half, parity):
        self.half, self.parity = half, parity

    def after(self, k):
        s = self.parity + k
        return Group(self.half + s // 2, s % 2)

    @property
    def n(self):
        return self.half * 2 + self.parity

    def batch(self, b):
        return self.half * 4 + (2 * self.parity + b)


def bass_gated_cross_attention_ternary_ffn(
    nc: bass.Bass, x, ctx_in, mask, g_xattn, g_ffn, wq, wk, wv, wo, w1, b1, w2, b2, out
):
    B, S, D = x.shape
    C = ctx_in.shape[2]
    FF = w1.shape[0]
    P = 128
    HD = D // HEADS
    KD = D // P
    C1 = C - P
    T = 2 * S
    NG = B // 2
    UH = 4
    UNITS = HEADS // UH
    VC = 2 * HD + 1
    FB = FF // P
    QB = 4
    NQ = B // QB
    SCALE = float(HD) ** -0.5
    HR = 3 * HD
    SR = HR + 2
    MAX_UNIT = 64.0
    LAG = 2
    HBUF = 4
    assert S == P and D == KD * P and 0 < C1 <= P and UH * S == 512 and B % 8 == 0 and FB % HBUF == 0

    x_v = x.rearrange("b s d -> s b d")
    out_v = out.rearrange("b s d -> s b d")
    ctx_v = ctx_in.rearrange("b s c -> s b c")

    with ExitStack() as top:
        def sem(name):
            return top.enter_context(nc.semaphore(name))

        def sb(name, shape, dt, where=top):
            return where.enter_context(nc.sbuf_tensor(name, shape, dt))

        xres = sb("xres", [P, B, D], F32)
        ident = sb("ident", [P, P], F32)
        ident16 = sb("ident16", [P, P], F16)
        ones = sb("ones", [P, P], F32)
        gates = sb("gates", [P, 4], F32)
        stats = sb("stats", [P, QB, 6], F32)
        meanvar = sb("meanvar", [P, QB, 2], F32)
        rstd = sb("rstd", [P, 4, QB], F32)
        gate_x, gate_f = gates[:, 2:3], gates[:, 3:4]

        one = ExitStack()
        wq_sb = sb("wq_sb", [P, KD, D], F32, one)
        wk_sb = sb("wk_sb", [P, 2, D], F32, one)
        wv_sb = sb("wv_sb", [P, 2, D], F32, one)
        wo_sb = sb("wo_sb", [P, KD, D], F32, one)
        maskT = sb("maskT", [P, B], F32, one)
        vmask = sb("vmask", [P, B], F32, one)
        escale = sb("escale", [P, B], F32, one)
        masks = [sb(f"masks{p}", [P, 4], F32, one) for p in range(2)]
        ctx_sb = [sb(f"ctx_sb{p}", [P, 2, C], F32, one) for p in range(2)]
        xln = sb("xln", [P, 2, D], F32, one)
        xlnT = sb("xlnT", [P, KD, T], F32, one)
        ctxT = [sb(f"ctxT{p}", [P, 2, T], F32, one) for p in range(2)]
        q16 = sb("q16", [P, 2, KD, T], F16, one)
        k16 = sb("k16", [P, 2, KD, T], F16, one)
        q_rows = [sb(f"q_rows{p}", [SR, HEADS, T], F16, one) for p in range(2)]
        k_rows = [sb(f"k_rows{p}", [64, HEADS, T], F16, one) for p in range(2)]
        v16 = [sb(f"v16_{p}", [P, 2, HEADS, VC], F16, one) for p in range(2)]
        prob = [sb(f"prob{p}", [P, UH * S], F32, one) for p in range(UNITS)]
        probl = [sb(f"probl{p}", [P, UH * S], F16, one) for p in range(UNITS)]
        wq_raw = prob[0][:].rearrange("p (k n) -> p k n", k=KD)
        wk_raw = prob[1][:].rearrange("p (k n) -> p k n", k=2)
        smax = sb("smax", [P, 2, HEADS], F32, one)
        smax16 = sb("smax16", [P, 2, 2 * HEADS], F16, one)
        smaxT = [sb(f"smaxT{p}", [2 * HEADS, S], F16, one) for p in range(2)]
        rsum = sb("rsum", [P, 2, HEADS], F32, one)
        attn = [sb(f"attn{p}", [P, HEADS, HD], F32, one) for p in range(2)]
        attnT = sb("attnT", [P, KD, S], F32, one)
        one.close()

        two = ExitStack()
        w1T = sb("w1T", [P, KD, FF], F16, two)
        w2T = sb("w2T", [P, FB, D], F16, two)
        w1_raw = sb("w1_raw", [P, FB, D], F32, two)
        w2_raw = sb("w2_raw", [P, KD, FF], F32, two)
        w_neg = sb("w_neg", [P, FB * D], F16, two)
        w1_t = sb("w1_t", [P, FB, D], F16, two)
        w2_t = sb("w2_t", [P, KD, FF], F16, two)
        wstat = sb("wstat", [P, 8], F32, two)
        b1_sb = sb("b1_sb", [P, FB], F32, two)
        b2_sb = sb("b2_sb", [P, D], F32, two)
        b2g = sb("b2g", [P, D], F32, two)
        yln = sb("yln", [P, QB, D], F32, two)
        y16 = [sb(f"y16_{p}", [P, 2, KD, QB * S], F16, two) for p in range(2)]
        hid = [sb(f"hid{p}", [P, QB * S], F32, two) for p in range(HBUF)]
        hidl = [sb(f"hidl{p}", [P, QB * S], F16, two) for p in range(HBUF)]
        ystage = [sb(f"ystage{p}", [P, QB, D], F32, two) for p in range(2)]
        two.close()

        bank = [top.enter_context(nc.psum_tensor(f"bank{i}", [P, 512], F32)) for i in range(8)]
        tr_bank, pj_bank = bank[0], bank[1]
        sm_bank, st_bank, pv_bank = bank[2:4], bank[4:6], bank[6:8]
        yt_bank, h_bank = bank[0:2], bank[2:4]
        y_bank = [bank[4:6], bank[6:8]]

        consts_set = sem("consts_set")
        weights_in = sem("weights_in")
        patterns_set = sem("patterns_set")
        mask_in = sem("mask_in")
        mask_f32 = sem("mask_f32")
        mask_transposed = sem("mask_transposed")
        mask_copied = sem("mask_copied")
        mask_counted = sem("mask_counted")
        mask_set = sem("mask_set")
        masks_picked, v_masked = sem("masks_picked"), sem("v_masked")
        gates_in = sem("gates_in")
        gates_set = sem("gates_set")
        x_in = [sem(f"x_in{p}") for p in range(2)]
        ctx_loaded = [sem(f"ctx_loaded{p}") for p in range(2)]
        ln_step = sem("ln_step")
        ln_ready, ln_done = sem("ln_ready"), sem("ln_done")
        x_transposed, xT_copied = sem("x_transposed"), sem("xT_copied")
        ctx_transposed, ctxT_copied = sem("ctx_transposed"), sem("ctxT_copied")
        q_made, q_high, q_split = sem("q_made"), sem("q_high"), sem("q_split")
        k_made, k_high, k_split = sem("k_made"), sem("k_high"), sem("k_split")
        v_made, v_high, v_split = sem("v_made"), sem("v_high"), sem("v_split")
        q_moved = [sem(f"q_moved{p}") for p in range(2)]
        k_moved = [sem(f"k_moved{p}") for p in range(2)]
        weights_permuted = sem("weights_permuted")
        rough_scored, max_taken = sem("rough_scored"), sem("max_taken")
        max_rounded, max_split = sem("max_rounded"), sem("max_split")
        max_transposed, maxT_copied = sem("max_transposed"), sem("maxT_copied")
        max_moved = [sem(f"max_moved{b}") for b in range(2)]
        scored, exp_done, prob_split = sem("scored"), sem("exp_done"), sem("prob_split")
        weighed, sums_inverted, norm_read, norm_done = (
            sem("weighed"), sem("sums_inverted"), sem("norm_read"), sem("norm_done"))
        attn_transposed, attnT_copied = sem("attn_transposed"), sem("attnT_copied")
        projected, x1_done = sem("projected"), sem("x1_done")

        ffn_in, ffn_b2_in = sem("ffn_in"), sem("ffn_b2_in")
        w_step, w_summed, w_ternary = sem("w_step"), sem("w_summed"), sem("w_ternary")
        w_transposed, wT_copied = sem("w_transposed"), sem("wT_copied")
        b2_scaled = sem("b2_scaled")
        y_step, y_ready, y_done = sem("y_step"), sem("y_ready"), sem("y_done")
        y_transposed, y_high, y_split = sem("y_transposed"), sem("y_high"), sem("y_split")
        biased = sem("biased")
        h_made, gelu_done, h_split = sem("h_made"), sem("gelu_done"), sem("h_split")
        h_used, y_made, y_added = sem("h_used"), sem("y_made"), sem("y_added")
        y_out = [sem(f"y_out{p}") for p in range(2)]

        NC_SETS = 5
        def move_parts(sp, g, parts, src, dst, moved):
            for i, part in enumerate(parts):
                sp.dma_start(dst[g.parity][i * HD:(i + 1) * HD], src[:, part]).then_inc(moved[g.parity], 16)

        def move_heads(sp, g, split, free):
            if free is not None:
                sp.wait_ge(scored, free)
            sp.wait_ge(k_split, split)
            move_parts(sp, g, (0, 0, 1), k16, k_rows, k_moved)
            sp.wait_ge(q_split, split)
            move_parts(sp, g, (0, 1, 0), q16, q_rows, q_moved)

        def move_max(sp, g, b, copied):
            sp.wait_ge(maxT_copied, copied)
            sp.dma_start(q_rows[g.parity][HR:SR, :, b * S:(b + 1) * S], smaxT[b][:]).then_inc(max_moved[b], 16)

        def load_x(sp, g):
            sp.dma_start(xres[:, bass.ds(g.batch(0), 2), :], x_v[:, bass.ds(g.batch(0), 2), :]).then_inc(
                x_in[g.parity], 16)

        def load_ctx(sp, g):
            sp.dma_start(ctx_sb[g.parity][:], ctx_v[:, bass.ds(g.batch(0), 2), :]).then_inc(
                ctx_loaded[g.parity], 16)

        def sp_group(sp, g, left):
            first = isinstance(g.half, int) and g.n == 0
            def held(value):
                return value if isinstance(value, int) else sp.snap(value)

            split = held(g.n + 2)
            scores_before = None if first else held(2 * UNITS * g.n)
            max_b1, max_b0 = held(g.batch(1) + 1), held(g.batch(0) + 3)
            x_past = held(2 * (g.n + 2))
            if left >= 3:
                sp.wait_ge(ln_done, x_past)
                load_x(sp, g.after(3))
                sp.wait_ge(ctx_transposed, split)
                load_ctx(sp, g.after(3))
            if left >= 1:
                move_heads(sp, g.after(1), split, scores_before)
            move_max(sp, g, 1, max_b1)
            if left >= 1:
                move_max(sp, g.after(1), 0, max_b0)

        def transpose_x(pe, g, tr_free):
            for busy in tr_free:
                pe.wait_ge(*busy)
            pe.wait_ge(ln_done, 2 * (g.n + 1))
            for k in range(KD):
                for b in range(2):
                    last = pe.transpose(tr_bank[:, k * T + b * S:k * T + (b + 1) * S],
                                        xln[:, b, k * P:(k + 1) * P], ident[:])
            last.then_inc(x_transposed, 1)
            return [(xT_copied, g.n + 1)]

        def transpose_ctx(pe, g, tr_free):
            for busy in tr_free:
                pe.wait_ge(*busy)
            pe.wait_ge(ctx_loaded[g.parity], 16 * (g.half + 1))
            for b in range(2):
                pe.transpose(tr_bank[:, b * S:(b + 1) * S], ctx_sb[g.parity][:, b, 0:P], ident[:])
            for b in range(2):
                last = pe.transpose(tr_bank[0:C1, T + b * S:T + (b + 1) * S],
                                    ctx_sb[g.parity][:, b, P:C], ident[:])
            last.then_inc(ctx_transposed, 1)
            return [(ctxT_copied, g.n + 1)]

        def project_q(pe, g, m):
            if m == 0:
                pe.wait_ge(xT_copied, g.n + 1)
            for k in range(KD):
                last = pe.matmul(pj_bank[:, m * T:(m + 1) * T], wq_sb[:, k, m * P:(m + 1) * P],
                                 xlnT[:, k, :], start=(k == 0), stop=(k == KD - 1))
            if m == KD - 1:
                last.then_inc(q_made, 1)

        def project_k(pe, g, pj_free):
            pe.wait_ge(*pj_free)
            pe.wait_ge(ctxT_copied, g.n + 1)
            for m in range(KD):
                for k, rows in enumerate((P, C1)):
                    last = pe.matmul(pj_bank[:, m * T:(m + 1) * T], wk_sb[0:rows, k, m * P:(m + 1) * P],
                                     ctxT[g.parity][0:rows, k, :], start=(k == 0), stop=(k == 1))
            last.then_inc(k_made, 1)
            return k_split, g.n + 1

        def project_v(pe, g, pj_free):
            pe.wait_ge(*pj_free)
            pe.wait_ge(ctxT_copied, g.n + 1)
            for b in range(2):
                for k, rows in enumerate((P, C1)):
                    last = pe.matmul(pj_bank[:, b * D:(b + 1) * D], ctxT[g.parity][0:rows, k, b * S:(b + 1) * S],
                                     wv_sb[0:rows, k, :], start=(k == 0), stop=(k == 1))
            last.then_inc(v_made, 1)
            return v_split, g.n + 1

        def rough_scores(pe, g, b, u):
            n = g.batch(b) * UNITS + u
            if not (isinstance(n, int) and n < 2):
                pe.wait_ge(max_taken, n - 1)
            if b == 0 and u == 0:
                pe.wait_ge(k_moved[g.parity], 16 * 3 * (g.half + 1))
                pe.wait_ge(q_moved[g.parity], 16 * 3 * (g.half + 1))
            cols = slice(b * S, (b + 1) * S)
            for c in range(UH):
                last = pe.matmul(sm_bank[u % 2][:, c * S:(c + 1) * S],
                                 q_rows[g.parity][0:HD, u * UH + c, cols],
                                 k_rows[g.parity][0:HD, u * UH + c, cols], start=True, stop=True)
            last.then_inc(rough_scored, 1)

        def transpose_max(pe, g, b, tr_free):
            for busy in tr_free:
                pe.wait_ge(*busy)
            n = g.batch(b)
            pe.wait_ge(max_split, n + 1)
            pe.transpose(tr_bank[0:2 * HEADS, 0:S // 2].bitcast(F16), smax16[:, b, :],
                         ident16[:]).then_inc(max_transposed, 1)
            return [(maxT_copied, n + 1)]

        def scores(pe, g, b, u):
            n = g.batch(b) * UNITS + u
            if u == 0:
                pe.wait_ge(max_moved[b], 16 * (g.n + 1))
            if not (isinstance(n, int) and n < 2):
                pe.wait_ge(exp_done, n - 1)
            cols = slice(b * S, (b + 1) * S)
            for c in range(UH):
                last = pe.matmul(st_bank[u % 2][:, c * S:(c + 1) * S],
                                 k_rows[g.parity][0:SR, u * UH + c, cols],
                                 q_rows[g.parity][0:SR, u * UH + c, cols], start=True, stop=True)
            last.then_inc(scored, 1)

        def weigh(pe, g, b, u):
            n = g.batch(b)
            half, c0 = u // 2, u % 2 * UH
            pe.wait_ge(prob_split, n * UNITS + (u + 1))
            if b == 0 and u == 0:
                pe.wait_ge(v_masked, g.n + 1)
                pe.wait_ge(v_split, g.n + 1)
            if u % 2 == 0 and not (isinstance(n, int) and n == 0):
                pe.wait_ge(norm_read, n * 2 + (half - 1))
            for c in range(UH):
                o = pv_bank[half][:, (c0 + c) * VC:(c0 + c + 1) * VC]
                v = v16[g.parity][:, b, u * UH + c, :]
                high = prob[u][:].bitcast(BF16)[:, 2 * c * S + 1:2 * (c + 1) * S:2]
                pe.matmul(o, high, v, start=True, stop=False)
                last = pe.matmul(o, probl[u][:, c * S:(c + 1) * S], v, start=False, stop=True)
            last.then_inc(weighed, 1)

        def transpose_attn(pe, n, b, tr_free):
            for busy in tr_free:
                pe.wait_ge(*busy)
            pe.wait_ge(norm_done, 2 * n + 2)
            for k in range(KD):
                last = pe.transpose(tr_bank[:, k * S:(k + 1) * S],
                                    attn[b][:].rearrange("p h d -> p (h d)")[:, k * P:(k + 1) * P], ident[:])
            last.then_inc(attn_transposed, 1)
            return [(attnT_copied, n + 1)]

        def project_out(pe, n, tr_free):
            for busy in tr_free:
                pe.wait_ge(*busy)
            pe.wait_ge(attnT_copied, n + 1)
            for k in range(KD):
                last = pe.matmul(tr_bank[:, 0:D], attnT[:, k, :], wo_sb[:, k, :], start=(k == 0),
                                 stop=(k == KD - 1))
            last.then_inc(projected, 1)
            return [(x1_done, n + 1)]

        def pe_first(pe):
            pe.wait_ge(consts_set, NC_SETS)
            pe.wait_ge(mask_f32, 1)
            pe.transpose(st_bank[0][:, 0:B], maskT[:], ident[:]).then_inc(mask_transposed, 1)
            pe.wait_ge(mask_copied, 1)
            pe.matmul(st_bank[1][:, 0:B], ones[:], vmask[:], start=True, stop=True).then_inc(mask_counted, 1)
            g0, g1 = Group(0, 0), Group(0, 1)
            pe.wait_ge(ln_done, 2)
            tr = transpose_x(pe, g0, [])
            pe.wait_ge(weights_in, 16 * 6)
            pe.wait_ge(weights_permuted, 4)
            for m in range(KD):
                project_q(pe, g0, m)
            tr = transpose_ctx(pe, g0, tr)
            pj = project_k(pe, g0, (q_split, 1))
            pj = project_v(pe, g0, pj)
            tr = transpose_ctx(pe, g1, tr)
            pj = project_k(pe, g1, pj)
            tr = transpose_x(pe, g1, tr)
            pe.wait_ge(*pj)
            for m in range(KD):
                project_q(pe, g1, m)
            for u in range(UNITS):
                rough_scores(pe, g0, 0, u)
            transpose_max(pe, g0, 0, tr)

        def pe_group(pe, g, left):
            first = isinstance(g.half, int) and g.n == 0
            g1, g2 = g.after(1), g.after(2)
            before = g.after(-1)
            tr = [(maxT_copied, 1)] if first else [(x1_done, g.batch(0) - 1)]
            rough_scores(pe, g, 1, 0)
            rough_scores(pe, g, 1, 1)
            scores(pe, g, 0, 0)
            if not first:
                weigh(pe, before, 1, 2)
            rough_scores(pe, g, 1, 2)
            scores(pe, g, 0, 1)
            if not first:
                weigh(pe, before, 1, 3)
            if left >= 2:
                tr = transpose_ctx(pe, g2, tr)
            rough_scores(pe, g, 1, 3)
            if left >= 1:
                project_v(pe, g1, (q_split, g.n + 2))
            scores(pe, g, 0, 2)
            weigh(pe, g, 0, 0)
            if not first:
                tr = transpose_attn(pe, g.batch(0) - 1, 1, tr)
            scores(pe, g, 0, 3)
            weigh(pe, g, 0, 1)
            tr = transpose_max(pe, g, 1, tr)
            if left >= 2:
                project_k(pe, g2, (v_split, g.n + 2))
            if not first:
                tr = project_out(pe, g.batch(0) - 1, tr)
            if left >= 1:
                rough_scores(pe, g1, 0, 0)
                rough_scores(pe, g1, 0, 1)
            scores(pe, g, 1, 0)
            weigh(pe, g, 0, 2)
            if left >= 1:
                rough_scores(pe, g1, 0, 2)
            scores(pe, g, 1, 1)
            weigh(pe, g, 0, 3)
            if left >= 2:
                tr = transpose_x(pe, g2, tr)
            if left >= 1:
                rough_scores(pe, g1, 0, 3)
            scores(pe, g, 1, 2)
            weigh(pe, g, 1, 0)
            tr = transpose_attn(pe, g.batch(0), 0, tr)
            scores(pe, g, 1, 3)
            weigh(pe, g, 1, 1)
            if left >= 1:
                tr = transpose_max(pe, g1, 0, tr)
            if left >= 2:
                pe.wait_ge(k_split, g.n + 3)
                for m in range(KD):
                    project_q(pe, g2, m)
            tr = project_out(pe, g.batch(0), tr)
            if left == 0:
                for u in range(2, UNITS):
                    weigh(pe, g, 1, u)
                tr = transpose_attn(pe, g.batch(1), 1, tr)
                project_out(pe, g.batch(1), tr)

        def apply_x(act, g):
            act.wait_ge(ln_ready, g.n + 1)
            if not (isinstance(g.half, int) and g.n == 0):
                act.wait_ge(x_transposed, g.n)
            for b in range(2):
                act.activation(xln[:, b, :], row_of(g.batch(b)), ACT.Identity, bias=rstd[:, 3, b:b + 1],
                               scale=rstd[:, 1, b:b + 1]).then_inc(ln_done, 1)

        def copy_xT(act, g):
            act.wait_ge(x_transposed, g.n + 1)
            if not (isinstance(g.half, int) and g.n == 0):
                act.wait_ge(q_made, g.n)
            act.copy(xlnT[:].rearrange("p k t -> p (k t)"), tr_bank[:]).then_inc(xT_copied, 1)

        def copy_ctxT(act, g):
            act.wait_ge(ctx_transposed, g.n + 1)
            if not (isinstance(g.half, int) and g.n < 2):
                act.wait_ge(v_made, g.n - 1)
            act.copy(ctxT[g.parity][:, 0, :], tr_bank[:, 0:T])
            act.copy(ctxT[g.parity][0:C1, 1, :], tr_bank[0:C1, T:2 * T]).then_inc(ctxT_copied, 1)

        def high_q(act, g):
            act.wait_ge(q_made, g.n + 1)
            if not (isinstance(g.half, int) and g.n == 0):
                before = Group(g.half - 1, 1) if g.parity == 0 else Group(g.half, 0)
                act.wait_ge(q_moved[before.parity], 16 * 3 * (before.half + 1))
            act.copy(q16[:, 0].rearrange("p k t -> p (k t)"), pj_bank[:]).then_inc(q_high, 1)

        def high_k(act, g):
            act.wait_ge(k_made, g.n + 1)
            if not (isinstance(g.half, int) and g.n == 0):
                before = Group(g.half - 1, 1) if g.parity == 0 else Group(g.half, 0)
                act.wait_ge(k_moved[before.parity], 16 * 3 * (before.half + 1))
            act.copy(k16[:, 0].rearrange("p k t -> p (k t)"), pj_bank[:]).then_inc(k_high, 1)

        def high_v(act, g):
            act.wait_ge(v_made, g.n + 1)
            if not (isinstance(g.half, int) and g.n < 2):
                act.wait_ge(weighed, 2 * UNITS * (g.n - 1))
            act.wait_ge(masks_picked, g.n + 1)
            for b in range(2):
                last = act.activation(v16[g.parity][:, b, :, 0:HD],
                                      pj_bank[:, b * D:(b + 1) * D].rearrange("p (h d) -> p h d", h=HEADS),
                                      ACT.Identity, bias=0.0, scale=masks[g.parity][:, b:b + 1])
            last.then_inc(v_high, 1)

        def copy_maxT(act, g, b):
            n = g.batch(b)
            act.wait_ge(max_transposed, n + 1)
            if not (isinstance(g.half, int) and g.n == 0):
                act.wait_ge(max_moved[b], 16 * g.n)
            act.copy(smaxT[b][:],
                     tr_bank[0:2 * HEADS, 0:S // 2].bitcast(F16)).then_inc(maxT_copied, 1)

        def exponentials(act, g, b, u):
            n = g.batch(b) * UNITS + u
            act.wait_ge(scored, n + 1)
            if not (isinstance(n, int) and n < UNITS):
                act.wait_ge(weighed, n - (UNITS - 1))
            act.activation(prob[u][:], st_bank[u % 2][:], ACT.Exp, bias=0.0,
                           scale=masks[g.parity][:, 2 + b:3 + b]).then_inc(exp_done, 1)

        def copy_attnT(act, n):
            act.wait_ge(attn_transposed, n + 1)
            if not (isinstance(n, int) and n == 0):
                act.wait_ge(projected, n)
            act.copy(attnT[:].rearrange("p k t -> p (k t)"), tr_bank[:, 0:KD * S]).then_inc(attnT_copied, 1)

        def act_first(act):
            act.wait_ge(gates_in, 32)
            act.activation(gates[:, 2:4], gates[:, 0:2], ACT.Tanh).then_inc(gates_set, 1)
            g0, g1 = Group(0, 0), Group(0, 1)
            apply_x(act, g0)
            copy_xT(act, g0)
            high_q(act, g0)
            copy_ctxT(act, g0)
            high_k(act, g0)
            high_v(act, g0)
            copy_ctxT(act, g1)
            high_k(act, g1)
            apply_x(act, g1)
            copy_xT(act, g1)
            high_q(act, g1)
            copy_maxT(act, g0, 0)

        def act_group(act, g, left):
            first = isinstance(g.half, int) and g.n == 0
            g1, g2 = g.after(1), g.after(2)
            exponentials(act, g, 0, 0)
            exponentials(act, g, 0, 1)
            if left >= 2:
                copy_ctxT(act, g2)
            if left >= 1:
                high_v(act, g1)
            exponentials(act, g, 0, 2)
            if not first:
                copy_attnT(act, g.batch(0) - 1)
            exponentials(act, g, 0, 3)
            copy_maxT(act, g, 1)
            if left >= 2:
                apply_x(act, g2)
                high_k(act, g2)
            exponentials(act, g, 1, 0)
            exponentials(act, g, 1, 1)
            if left >= 2:
                copy_xT(act, g2)
            exponentials(act, g, 1, 2)
            copy_attnT(act, g.batch(0))
            exponentials(act, g, 1, 3)
            if left >= 1:
                copy_maxT(act, g1, 0)
            if left >= 2:
                high_q(act, g2)
            if left == 0:
                copy_attnT(act, g.batch(1))

        def ln_part(dve, i, rows, step, base, ready):
            n = len(rows)
            half, y, t, shift = (rstd[:, k, 0:n] for k in range(4))
            if i > 0:
                dve.wait_ge(step, base + i)
            if i == 0:
                for b, row in enumerate(rows):
                    last = dve.bn_stats(stats[:, b, :], row)
            elif i == 1:
                dve.tensor_copy(t, stats[:, 0:n, 1])
                for b in range(n):
                    last = dve.bn_aggr(meanvar[:, b, :], stats[:, b, :])
            elif i == 2:
                last = dve.tensor_scalar(t, meanvar[:, 0:n, 1], EPS, None, ALU.add)
            elif i == 3:
                dve.tensor_scalar(y.bitcast(I32), t.bitcast(I32), -0.5, RSQRT_SEED, ALU.mult, ALU.add)
                last = dve.tensor_scalar(half, t, -0.5, None, ALU.mult)
            elif i == LN_PARTS - 1:
                dve.scalar_tensor_tensor(shift, meanvar[:, 0:n, 0], -1.0, y, ALU.mult,
                                         ALU.mult).then_inc(ready, 1)
                return
            elif i % 3 == 1:
                last = dve.tensor_tensor(t, y, y, ALU.mult)
            elif i % 3 == 2:
                last = dve.tensor_tensor(t, t, half, ALU.mult)
            else:
                last = dve.scalar_tensor_tensor(y, t, 1.5, y, ALU.add, ALU.mult)
            last.then_inc(step, 1)

        def row_of(batch):
            return xres[:, bass.ds(batch, 1), :].rearrange("p o d -> p (o d)")

        def norm_x(dve, g, parts):
            for i in parts:
                if i == 0:
                    dve.wait_ge(x_in[g.parity], 16 * (g.half + 1))
                if i == 3 and not (isinstance(g.half, int) and g.n == 0):
                    dve.wait_ge(ln_done, 2 * g.n)
                rows = [row_of(g.batch(b)) for b in range(2)] if i == 0 else (None,) * 2
                ln_part(dve, i, rows, ln_step, g.n * (LN_PARTS - 1), ln_ready)

        def low_q(dve, g):
            dve.wait_ge(q_high, g.n + 1)
            dve.tensor_tensor(q16[:, 1].rearrange("p k t -> p (k t)"), pj_bank[:],
                              q16[:, 0].rearrange("p k t -> p (k t)"),
                              ALU.subtract).then_inc(q_split, 1)

        def low_k(dve, g):
            dve.wait_ge(k_high, g.n + 1)
            dve.tensor_tensor(k16[:, 1].rearrange("p k t -> p (k t)"), pj_bank[:],
                              k16[:, 0].rearrange("p k t -> p (k t)"),
                              ALU.subtract).then_inc(k_split, 1)

        def pick_masks(pool, g):
            if not (isinstance(g.half, int) and g.n < 2):
                pool.wait_ge(weighed, 2 * UNITS * (g.n - 1))
            for c, source in ((0, vmask), (2, escale)):
                last = pool.tensor_tensor(masks[g.parity][:, c:c + 2], source[:, bass.ds(g.batch(0), 2)],
                                          ones[:, 0:2], ALU.mult)
            last.then_inc(masks_picked, 1)
            pool.wait_ge(masks_picked, g.n + 1)
            for b in range(2):
                last = pool.tensor_tensor(v16[g.parity][:, b, :, 2 * HD], ones[:, 0:HEADS],
                                          masks[g.parity][:, b:b + 1].to_broadcast([P, HEADS]), ALU.mult)
            last.then_inc(v_masked, 1)

        def low_v(dve, g):
            dve.wait_ge(v_high, g.n + 1)
            for b in range(2):
                last = dve.scalar_tensor_tensor(
                    v16[g.parity][:, b, :, HD:2 * HD],
                    pj_bank[:, b * D:(b + 1) * D].rearrange("p (h d) -> p h d", h=HEADS),
                    masks[g.parity][:, b:b + 1], v16[g.parity][:, b, :, 0:HD], ALU.mult, ALU.subtract)
            last.then_inc(v_split, 1)

        def take_max(dve, g, b, u):
            n = g.batch(b) * UNITS + u
            dve.wait_ge(rough_scored, n + 1)
            dve.tensor_reduce(smax[:, b, u * UH:(u + 1) * UH],
                              sm_bank[u % 2][:].rearrange("p (h j) -> p h j", h=UH), AX.X,
                              ALU.max).then_inc(max_taken, 1)

        def split_max(dve, g, b, between=None):
            n = g.batch(b)
            dve.wait_ge(max_taken, (n + 1) * UNITS)
            dve.tensor_scalar(smax16[:, b, 0:HEADS], smax[:, b, :], 1.0 / MAX_UNIT, None,
                              ALU.mult).then_inc(max_rounded, 1)
            if between:
                between[0](between[1])
            dve.wait_ge(max_rounded, n + 1)
            dve.scalar_tensor_tensor(smax16[:, b, HEADS:2 * HEADS], smax[:, b, :], 1.0 / MAX_UNIT,
                                     smax16[:, b, 0:HEADS], ALU.mult, ALU.subtract).then_inc(max_split, 1)

        def normalise(dve, n, b, half, between=None):
            hb = HEADS // 2
            heads = slice(half * hb, (half + 1) * hb)
            dve.wait_ge(weighed, n * UNITS + 2 * (half + 1))
            if not (isinstance(n, int) and n < 2):
                dve.wait_ge(attn_transposed, n - 1)
            pv = pv_bank[half][:, 0:hb * VC].rearrange("p (h c) -> p h c", h=hb)
            dve.reciprocal(rsum[:, b, heads], pv[:, :, 2 * HD])
            dve.tensor_reduce(attn[b][:, heads, :],
                              pv[:, :, 0:2 * HD].rearrange("p h (two d) -> p h d two", two=2), AX.X,
                              ALU.add).then_inc(norm_read, 1)
            if between:
                between[0](between[1])
            dve.wait_ge(norm_read, n * 2 + (half + 1))
            dve.tensor_tensor(attn[b][:, heads, :], attn[b][:, heads, :],
                              rsum[:, b, heads].unsqueeze(2).to_broadcast([P, hb, HD]),
                              ALU.mult).then_inc(norm_done, 1)

        def add_attention(dve, n):
            dve.wait_ge(projected, n + 1)
            row = xres[:, bass.ds(n, 1), :].rearrange("p o d -> p (o d)")
            dve.scalar_tensor_tensor(row, tr_bank[:, 0:D], gate_x, row, ALU.mult, ALU.add).then_inc(x1_done, 1)

        def dve_first(dve):
            for p in range(2):
                dve.memset(k_rows[p][32:64].rearrange("p h t -> p (h t)"), -MAX_UNIT).then_inc(consts_set, 1)
            dve.memset(ones[:], 1.0).then_inc(consts_set, 1)
            dve.wait_ge(mask_in, 16)
            dve.tensor_copy(maskT[:], escale[:].bitcast(U8)[:, 0:B]).then_inc(mask_f32, 1)
            g0, g1 = Group(0, 0), Group(0, 1)
            norm_x(dve, g0, range(LN_PARTS))
            dve.wait_ge(weights_in, 16 * 6)
            for raw, w in ((wq_raw, wq_sb), (wk_raw, wk_sb)):
                for k in range(2):
                    rows = C1 if raw is wk_raw and k == 1 else P
                    for m in range(KD):
                        last = dve.tensor_copy(
                            w[0:rows, k, m * P:(m + 1) * P].rearrange("p (d j) -> p d j", d=HD),
                            raw[0:rows, k, :].rearrange("p (j m d) -> p m d j", m=KD, d=HD)[:, m])
                    last.then_inc(weights_permuted, 1)
            dve.wait_ge(mask_transposed, 1)
            dve.tensor_copy(vmask[:], st_bank[0][:, 0:B]).then_inc(mask_copied, 1)
            dve.wait_ge(mask_counted, 1)
            dve.tensor_scalar(maskT[:], st_bank[1][:, 0:B], 0.5, None, ALU.is_lt)
            dve.tensor_scalar(escale[:], st_bank[1][:, 0:B], 0.5, SCALE, ALU.is_gt, ALU.mult).then_inc(mask_f32, 1)
            dve.wait_ge(mask_f32, 2)
            dve.tensor_tensor(vmask[:], vmask[:], maskT[:], ALU.max).then_inc(mask_set, 1)
            dve.wait_ge(mask_set, 1)
            dve.wait_ge(gates_set, 1)
            low_q(dve, g0)
            low_k(dve, g0)
            low_v(dve, g0)
            norm_x(dve, g1, range(LN_PARTS))
            low_k(dve, g1)
            low_q(dve, g1)
            for u in range(UNITS):
                take_max(dve, g0, 0, u)
            split_max(dve, g0, 0)
            norm_x(dve, g0.after(2), range(0, LN_B))

        def dve_group(dve, g, left):
            first = isinstance(g.half, int) and g.n == 0
            g1, g2, g3 = g.after(1), g.after(2), g.after(3)

            def norm(i):
                if i < LN_B and left >= 3:
                    norm_x(dve, g3, (i,))
                if i >= LN_B and left >= 2:
                    norm_x(dve, g2, (i,))

            take_max(dve, g, 1, 0)
            if not first:
                add_attention(dve, g.batch(0) - 2)
            take_max(dve, g, 1, 1)
            norm(8)
            if not first:
                normalise(dve, g.batch(0) - 1, 1, 1)
            norm(9)
            take_max(dve, g, 1, 2)
            norm(10)
            take_max(dve, g, 1, 3)
            split_max(dve, g, 1, (norm, 11))
            norm(12)
            if left >= 1:
                low_v(dve, g1)
            norm(13)
            normalise(dve, g.batch(0), 0, 0, (norm, 0))
            if left >= 2:
                low_k(dve, g2)
            norm(1)
            if left >= 1:
                take_max(dve, g1, 0, 0)
            if not first:
                add_attention(dve, g.batch(0) - 1)
            norm(2)
            if left >= 1:
                take_max(dve, g1, 0, 1)
            norm(3)
            normalise(dve, g.batch(0), 0, 1, (norm, 4))
            if left >= 1:
                take_max(dve, g1, 0, 2)
                norm(5)
                take_max(dve, g1, 0, 3)
                split_max(dve, g1, 0, (norm, 6))
            normalise(dve, g.batch(1), 1, 0, (norm, 7))
            if left >= 2:
                low_q(dve, g2)
            if left == 0:
                add_attention(dve, g.batch(0))
            if left == 0:
                normalise(dve, g.batch(1), 1, 1)
                add_attention(dve, g.batch(1))

        def low_prob(pool, g, b, u):
            n = g.batch(b) * UNITS + u
            pool.wait_ge(exp_done, n + 1)
            pool.tensor_tensor(probl[u][:], prob[u][:], prob[u][:].bitcast(BF16)[:, 1::2],
                               ALU.subtract).then_inc(prob_split, 1)

        def pool_group(pool, g, left):
            for b in range(2):
                for u in range(UNITS):
                    low_prob(pool, g, b, u)
                    if b == 0 and u == 0 and left >= 1:
                        pick_masks(pool, g.after(1))

        def over_pairs(engine, do, pairs, apart=1):
            for s in range(2):
                do(engine, Group(0, s), 2 * pairs - 1 - s)
            with engine.Fori(1, pairs - apart) as i:
                for s in range(2):
                    do(engine, Group(i, s), 2 * apart + 1 - s)
            for r in range(pairs - apart, pairs):
                for s in range(2):
                    do(engine, Group(r, s), 2 * (pairs - r) - 1 - s)

        def over_groups(engine, do, apart=1):
            over_pairs(engine, do, NG // 2, apart)

        def steps(engine, do):
            over_pairs(engine, do, NQ // 2)

        def prepare_weights_dve(dve):
            dve.wait_ge(ffn_in, 16 * 3)
            for i, raw in enumerate((w1_raw, w2_raw)):
                dve.tensor_reduce(wstat[:, i:i + 1], raw[:].rearrange("p a b -> p (a b)"), AX.X, ALU.add,
                                  apply_absolute_value=True).then_inc(w_step, 1)
            dve.wait_ge(w_summed, 1)
            half_mean = 0.5 / float(FF * D)
            dve.tensor_scalar(wstat[:, 2:4], h_bank[0][:, 0:2], half_mean, 0.5e-8, ALU.mult,
                              ALU.max).then_inc(w_step, 1)
            dve.wait_ge(w_step, 3)
            dve.tensor_scalar(wstat[:, 4:6], wstat[:, 2:4], -1.0, None, ALU.mult).then_inc(w_step, 1)
            dve.wait_ge(w_step, 4)
            for i, (raw, tern) in enumerate(((w1_raw, w1_t), (w2_raw, w2_t))):
                flat = raw[:].rearrange("p a b -> p (a b)")
                dve.tensor_scalar(w_neg[:], flat, wstat[:, 4 + i:5 + i], None, ALU.is_lt).then_inc(w_step, 1)
                dve.wait_ge(w_step, 5 + i)
                dve.scalar_tensor_tensor(tern[:].rearrange("p a b -> p (a b)"), flat, wstat[:, 2 + i:3 + i],
                                         w_neg[:], ALU.is_gt, ALU.subtract).then_inc(w_ternary, 1)
                dve.wait_ge(w_ternary, 1 + i)
            dve.wait_ge(ffn_b2_in, 16)
            dve.tensor_scalar(b2g[:], b2_sb[:], gate_f, None, ALU.mult).then_inc(b2_scaled, 1)

        def prepare_weights_pe(pe):
            pe.wait_ge(w_step, 2)
            pe.wait_ge(x1_done, B)
            pe.matmul(h_bank[0][:, 0:2], ones[:], wstat[:, 0:2], start=True, stop=True).then_inc(w_summed, 1)
            n = 0
            for i, (tern, rows, cols) in enumerate(((w1_t, FB, KD), (w2_t, KD, FB))):
                pe.wait_ge(w_ternary, i + 1)
                for c in range(cols):
                    for r in range(rows):
                        q, o = n // 8, n % 8
                        if o == 0 and q >= 2:
                            pe.wait_ge(wT_copied, q - 1)
                        last = pe.transpose(y_bank[0][q % 2][:].bitcast(F16)[:, o * P:(o + 1) * P],
                                            tern[:, r, c * P:(c + 1) * P], ident16[:])
                        n += 1
                        if o == 7:
                            last.then_inc(w_transposed, 1)

        def prepare_weights_act(act):
            flat = [w1T[:, k, :] for k in range(KD)] + [
                w2T[:, 4 * q:4 * q + 4, :].rearrange("p f d -> p (f d)") for q in range(FB // 4)]
            for q, dst in enumerate(flat):
                act.wait_ge(w_transposed, q + 1)
                act.copy(dst, y_bank[0][q % 2][:].bitcast(F16)).then_inc(wT_copied, 1)

        def norm_y(dve, g, parts):
            for i in parts:
                if i == 3 and not (isinstance(g.half, int) and g.n == 0):
                    dve.wait_ge(y_done, QB * g.n)
                rows = [row_of(g.n * QB + b) for b in range(QB)] if i == 0 else (None,) * QB
                ln_part(dve, i, rows, y_step, g.n * (LN_PARTS - 1), y_ready)

        def apply_y(act, g):
            act.wait_ge(y_ready, g.n + 1)
            if not (isinstance(g.half, int) and g.n == 0):
                act.wait_ge(y_transposed, KD * g.n)
            for b in range(QB):
                act.activation(yln[:, b, :], row_of(g.n * QB + b), ACT.Identity, bias=rstd[:, 3, b:b + 1],
                               scale=rstd[:, 1, b:b + 1]).then_inc(y_done, 1)

        def transpose_y(pe, g):
            pe.wait_ge(y_done, QB * (g.n + 1))
            for k in range(KD):
                if not (isinstance(g.half, int) and g.n == 0):
                    pe.wait_ge(y_split, KD * g.n)
                for b in range(QB):
                    last = pe.transpose(yt_bank[k][:, b * S:(b + 1) * S], yln[:, b, k * P:(k + 1) * P], ident[:])
                last.then_inc(y_transposed, 1)

        def high_y(act, g):
            for k in range(KD):
                act.wait_ge(y_transposed, KD * g.n + (k + 1))
                if k == 0 and not (isinstance(g.half, int) and g.n < 2):
                    act.wait_ge(h_made, FB * (g.n - 1))
                act.copy(y16[g.parity][:, 0, k, :], yt_bank[k][:]).then_inc(y_high, 1)

        def low_y(dve, g):
            for k in range(KD):
                dve.wait_ge(y_high, KD * g.n + (k + 1))
                dve.tensor_tensor(y16[g.parity][:, 1, k, :], yt_bank[k][:], y16[g.parity][:, 0, k, :],
                                  ALU.subtract).then_inc(y_split, 1)

        def hidden(pe, g, f):
            n = g.n * FB + f
            if f == 0:
                pe.wait_ge(y_split, KD * (g.n + 1))
            if not (isinstance(n, int) and n < 2):
                pe.wait_ge(gelu_done, n - 1)
            i = 0
            for k in range(KD):
                for part in range(2):
                    last = pe.matmul(h_bank[f % 2][:], w1T[:, k, f * P:(f + 1) * P], y16[g.parity][:, part, k, :],
                                     start=(i == 0), stop=(i == 2 * KD - 1))
                    i += 1
            last.then_inc(h_made, 1)

        def gelu(act, g, f):
            n = g.n * FB + f
            act.wait_ge(h_made, n + 1)
            if not (isinstance(n, int) and n < HBUF):
                act.wait_ge(h_used, n - (HBUF - 1))
            act.activation(hid[f % HBUF][:], h_bank[f % 2][:], ACT.Gelu, bias=b1_sb[:, f:f + 1]).then_inc(gelu_done, 1)

        def low_h(dve, g, f):
            n = g.n * FB + f
            dve.wait_ge(gelu_done, n + 1)
            dve.tensor_tensor(hidl[f % HBUF][:], hid[f % HBUF][:], hid[f % HBUF][:].bitcast(BF16)[:, 1::2],
                              ALU.subtract).then_inc(h_split, 1)

        def second(pe, g, f):
            n = g.n * FB + f
            if f == 0 and not (isinstance(g.half, int) and g.n < 2):
                pe.wait_ge(y_added, QB * (g.n - 1))
            pe.wait_ge(h_split, n + 1)
            for b in range(QB):
                o = y_bank[g.parity][b // 2][:, (b % 2) * D:(b % 2 + 1) * D]
                high = hid[f % HBUF][:].bitcast(BF16)[:, 2 * b * S + 1:2 * (b + 1) * S:2]
                pe.matmul(o, high, w2T[:, f, :], start=(f == 0 and b % 2 == 0), stop=False, skip_group_check=True)
                last = pe.matmul(o, hidl[f % HBUF][:, b * S:(b + 1) * S], w2T[:, f, :], start=False,
                                 stop=(f == FB - 1), skip_group_check=True)
            last.then_inc(h_used, 1)

        def pe_step(pe, g, left):
            first = isinstance(g.half, int) and g.n == 0
            for f in range(FB):
                hidden(pe, g, f)
                if f >= LAG:
                    second(pe, g, f - LAG)
                elif not first:
                    second(pe, Group(g.half - 1, 1) if g.parity == 0 else Group(g.half, 0), FB - LAG + f)
                if f == FB // 2 + 1 and left >= 1:
                    transpose_y(pe, g.after(1))
            if left == 0:
                for f in range(FB - LAG, FB):
                    second(pe, g, f)

        def act_step(act, g, left):
            for f in range(FB):
                gelu(act, g, f)
                if f == FB // 2 - 1 and left >= 1:
                    apply_y(act, g.after(1))
                if f == FB // 2 + 1 and left >= 1:
                    high_y(act, g.after(1))

        def add_y(dve, g):
            dve.wait_ge(h_used, FB * (g.n + 1))
            dve.wait_ge(biased, g.n + 1)
            if not (isinstance(g.half, int) and g.n < 2):
                dve.wait_ge(y_out[g.parity], 16 * g.half)
            for b in range(QB):
                o = y_bank[g.parity][b // 2][:, (b % 2) * D:(b % 2 + 1) * D]
                dve.scalar_tensor_tensor(ystage[g.parity][:, b, :], o, gate_f,
                                         xres[:, bass.ds(g.n * QB + b, 1), :].rearrange("p o d -> p (o d)"),
                                         ALU.mult, ALU.add).then_inc(y_added, 1)

        def dve_step(dve, g, left):
            first = isinstance(g.half, int) and g.n == 0
            for f in range(FB):
                low_h(dve, g, f)
                if f < 4 and left >= 1:
                    norm_y(dve, g.after(1), (range(0, 2), range(2, 8), range(8, LN_PARTS - 1),
                                             range(LN_PARTS - 1, LN_PARTS))[f])
                if f == LAG and not first:
                    add_y(dve, Group(g.half - 1, 1) if g.parity == 0 else Group(g.half, 0))
                if f == FB // 2 + 1 and left >= 1:
                    low_y(dve, g.after(1))
            if left == 0:
                add_y(dve, g)

        def pool_step(pool, g, left):
            pool.wait_ge(y_done, QB * (g.n + 1))
            rows = xres[:, bass.ds(g.n * QB, QB), :]
            pool.tensor_tensor(rows, rows, b2g[:].unsqueeze(1).to_broadcast([P, QB, D]), ALU.add).then_inc(biased, 1)

        def sp_step(sp, g, left):
            sp.wait_ge(y_added, QB * (g.n + 1))
            sp.dma_start(out_v[:, bass.ds(g.n * QB, QB), :], ystage[g.parity][:]).then_inc(y_out[g.parity], 16)

        block = top.enter_context(nc.Block())

        @block.sync
        def _(sp):
            sp.dma_start(escale[:].bitcast(U8)[:, 0:S], mask).then_inc(mask_in, 16)
            load_x(sp, Group(0, 0))
            load_ctx(sp, Group(0, 0))
            load_x(sp, Group(0, 1))
            sp.dma_start(wq_raw, wq.rearrange("(k p) n -> p k n", p=P)).then_inc(weights_in, 16)
            sp.dma_start(wk_raw[:, 0, :], wk[0:P, :]).then_inc(weights_in, 16)
            sp.dma_start(wk_raw[0:C1, 1, :], wk[P:C, :]).then_inc(weights_in, 16)
            sp.dma_start(wv_sb[:, 0, :], wv[0:P, :]).then_inc(weights_in, 16)
            sp.dma_start(wv_sb[0:C1, 1, :], wv[P:C, :]).then_inc(weights_in, 16)
            sp.dma_start(wo_sb[:], wo.rearrange("(k p) n -> p k n", p=P)).then_inc(weights_in, 16)
            load_ctx(sp, Group(0, 1))
            sp.dma_start(gates[:, 0:1], g_xattn.partition_broadcast(P)).then_inc(gates_in, 16)
            sp.dma_start(gates[:, 1:2], g_ffn.partition_broadcast(P)).then_inc(gates_in, 16)
            sp.wait_ge(ln_done, 2)
            load_x(sp, Group(1, 0))
            sp.wait_ge(ctx_transposed, 1)
            load_ctx(sp, Group(1, 0))
            sp.wait_ge(consts_set, NC_SETS)
            move_heads(sp, Group(0, 0), 1, None)
            move_max(sp, Group(0, 0), 0, 1)
            over_groups(sp, sp_group, 2)
            sp.wait_ge(x1_done, B)
            sp.dma_start(w1_raw[:], w1.rearrange("(f p) d -> p f d", p=P)).then_inc(ffn_in, 16)
            sp.dma_start(w2_raw[:], w2.rearrange("(k p) f -> p k f", p=P)).then_inc(ffn_in, 16)
            with nc.allow_non_contiguous_dma(reason="1024 biases, one a row"):
                sp.dma_start(b1_sb[:], b1.rearrange("(f p) -> p f", p=P)).then_inc(ffn_in, 16)
            sp.dma_start(b2_sb[:], b2.partition_broadcast(P)).then_inc(ffn_b2_in, 16)
            steps(sp, sp_step)
            for p in range(2):
                sp.wait_ge(y_out[p], 16 * (NQ // 2))

        @block.gpsimd
        def _(pool):
            pool.memset(ident[:], 0.0).then_inc(consts_set, 1)
            pool.wait_ge(consts_set, 4)
            pool.affine_select(out=ident[:], in_=ident[:], compare_op=ALU.not_equal, fill=1.0, base=0,
                               pattern=[[-1, P]], channel_multiplier=1).then_inc(patterns_set, 1)
            pool.wait_ge(patterns_set, 1)
            pool.tensor_copy(ident16[:], ident[:]).then_inc(consts_set, 1)
            pool.wait_ge(mask_set, 1)
            pick_masks(pool, Group(0, 0))
            over_groups(pool, pool_group)
            pool.wait_ge(b2_scaled, 1)
            steps(pool, pool_step)

        @block.tensor
        def _(pe):
            pe_first(pe)
            over_groups(pe, pe_group)
            prepare_weights_pe(pe)
            transpose_y(pe, Group(0, 0))
            pe.wait_ge(wT_copied, 4)
            steps(pe, pe_step)

        @block.scalar
        def _(act):
            act_first(act)
            over_groups(act, act_group)
            prepare_weights_act(act)
            apply_y(act, Group(0, 0))
            high_y(act, Group(0, 0))
            steps(act, act_step)

        @block.vector
        def _(dve):
            dve_first(dve)
            over_groups(dve, dve_group, 2)
            dve.wait_ge(x1_done, B)
            prepare_weights_dve(dve)
            norm_y(dve, Group(0, 0), range(LN_PARTS))
            low_y(dve, Group(0, 0))
            steps(dve, dve_step)


_INS = ["x", "ctx_768", "mask_BxS2_bf1", "g_xattn", "g_ffn", "L0_xattn_Wq", "L0_xattn_Wk", "L0_xattn_Wv",
        "L0_xattn_Wo", "L0_ffn_W1", "L0_ffn_b1", "L0_ffn_W2", "L0_ffn_b2"]
_OUTS = [((128, 128, 256), "float32")]


def kernel(**inputs):
    import numpy as _np
    import concourse.bacc as _bacc
    from concourse import mybir as _mybir
    from concourse.bass_utils import run_bass_kernel_spmd as _run

    nc = _bacc.Bacc("TRN2", target_bir_lowering=False, num_devices=1)
    arrays, args = {}, []
    for name in _INS:
        a = _np.ascontiguousarray(inputs[name])
        arrays[f"in_{name}_dram"] = a
        args.append(nc.dram_tensor(f"in_{name}_dram", a.shape, _mybir.dt.from_np(a.dtype), kind="ExternalInput").ap())
    for i, (shape, dtype) in enumerate(_OUTS):
        dt = _mybir.dt.from_np(_np.dtype(dtype))
        args.append(nc.dram_tensor(f"out_{i}_dram", shape, dt, kind="ExternalOutput").ap())
    bass_gated_cross_attention_ternary_ffn(nc, *args)
    r = _run(nc, [arrays], core_ids=[0])
    got = tuple(r.results[0][f"out_{i}_dram"] for i in range(len(_OUTS)))
    return got[0]
```

```python
from contextlib import ExitStack

import concourse.bass as bass
from concourse import mybir

F32 = mybir.dt.float32
F16 = mybir.dt.float16
BF16 = mybir.dt.bfloat16
I32 = mybir.dt.int32
U8 = mybir.dt.uint8
ACT = mybir.ActivationFunctionType
ALU = mybir.AluOpType
AX = mybir.AxisListType

HEADS = 16
EPS = 1e-5
NEWTON = 3
RSQRT_SEED = float(0x5F3759DF)
LN_PARTS = 5 + 3 * NEWTON
LN_AHEAD = 8


class Group:

    def __init__(self, half, parity):
        self.half, self.parity = half, parity

    def after(self, k):
        s = self.parity + k
        return Group(self.half + s // 2, s % 2)

    @property
    def n(self):
        return self.half * 2 + self.parity

    def batch(self, b):
        return self.half * 4 + (2 * self.parity + b)


def bass_gated_cross_attention_ternary_ffn(
    nc: bass.Bass, x, ctx_in, mask, g_xattn, g_ffn, wq, wk, wv, wo, w1, b1, w2, b2, out
):
    B, S, D = x.shape
    C = ctx_in.shape[2]
    FF = w1.shape[0]
    P = 128
    HD = D // HEADS
    KD = D // P
    C1 = C - P
    T = 2 * S
    NG = B // 2
    UH = 4
    UNITS = HEADS // UH
    VC = 2 * HD + 1
    FB = FF // P
    QB = 4
    NQ = B // QB
    SCALE = float(HD) ** -0.5
    HR = 3 * HD
    SR = HR + 2
    MAX_UNIT = 64.0
    LAG = 2
    HBUF = 4
    assert S == P and D == KD * P and 0 < C1 <= P and UH * S == 512 and B % 8 == 0 and FB % HBUF == 0

    x_v = x.rearrange("b s d -> s b d")
    out_v = out.rearrange("b s d -> s b d")
    ctx_v = ctx_in.rearrange("b s c -> s b c")

    with ExitStack() as top:
        def sem(name):
            return top.enter_context(nc.semaphore(name))

        def sb(name, shape, dt, where=top):
            return where.enter_context(nc.sbuf_tensor(name, shape, dt))

        xres = sb("xres", [P, B, D], F32)
        ident = sb("ident", [P, P], F32)
        ident16 = sb("ident16", [P, P], F16)
        ones = sb("ones", [P, P], F32)
        gates = sb("gates", [P, 4], F32)
        stats = sb("stats", [P, QB, 6], F32)
        meanvar = sb("meanvar", [P, QB, 2], F32)
        rstd = sb("rstd", [P, 4, QB], F32)
        wstat = sb("wstat", [P, 8], F32)
        gate_x, gate_f = gates[:, 2:3], gates[:, 3:4]

        one = ExitStack()
        q_rows, k_rows = [None] * 2, [None] * 2
        for p in range(2):
            q_rows[p] = sb(f"q_rows{p}", [SR, 2, HEADS, S], F16, one)
            k_rows[p] = sb(f"k_rows{p}", [64, 2, HEADS, S], F16, one)
        wq_sb = sb("wq_sb", [P, KD, D], F32, one)
        wk_sb = sb("wk_sb", [P, 2, D], F32, one)
        wv_sb = sb("wv_sb", [P, 2, D], F32, one)
        wo_sb = sb("wo_sb", [P, KD, D], F32, one)
        vmask = sb("vmask", [P, B], F32, one)
        escale = sb("escale", [P, B], F32, one)
        masks = [sb(f"masks{p}", [P, 4], F32, one) for p in range(2)]
        ctx_sb = [sb(f"ctx_sb{p}", [P, 2, C], F32, one) for p in range(2)]
        xln = sb("xln", [P, 2, D], F32, one)
        xlnT = sb("xlnT", [P, KD, T], F32, one)
        ctxT = [sb(f"ctxT{p}", [P, 2, T], F32, one) for p in range(2)]
        q16 = [sb(f"q16_{p}", [P, 2, 2, KD, S], F16, one) for p in range(2)]
        k16 = sb("k16", [P, 2, 2, KD, S], F16, one)
        v16 = [sb(f"v16_{p}", [P, 2, HEADS, VC], F16, one) for p in range(2)]
        prob = [sb(f"prob{p}", [P, UH * S], F32, one) for p in range(UNITS)]
        probl = [sb(f"probl{p}", [P, UH * S], F16, one) for p in range(UNITS)]
        wq_raw = prob[0][:].rearrange("p (k n) -> p k n", k=KD)
        wk_raw = prob[1][:].rearrange("p (k n) -> p k n", k=2)
        smax = sb("smax", [P, 2, HEADS], F32, one)
        smax16 = sb("smax16", [P, 2, 2 * HEADS], F16, one)
        smaxT = [sb(f"smaxT{p}", [2 * HEADS, S], F16, one) for p in range(2)]
        rsum = sb("rsum", [P, 2, HEADS], F32, one)
        attn = [sb(f"attn{p}", [P, HEADS, HD], F32, one) for p in range(2)]
        attnT = sb("attnT", [P, KD, S], F32, one)
        maskT = attnT[:, 0, :]
        one.close()

        two = ExitStack()
        w1_raw = sb("w1_raw", [P, FB, D], F32, two)
        w2_raw = sb("w2_raw", [P, KD, FF], F32, two)
        w_neg = sb("w_neg", [P, FB * D], F16, two)
        w1_t = sb("w1_t", [P, FB, D], F16, two)
        w2_t = sb("w2_t", [P, KD, FF], F16, two)
        w1T = sb("w1T", [P, KD, FF], F16, two)
        w2T = sb("w2T", [P, FB, D], F16, two)
        b1_sb = sb("b1_sb", [P, FB], F32, two)
        b2_sb = sb("b2_sb", [P, D], F32, two)
        b2g = sb("b2g", [P, D], F32, two)
        yln = sb("yln", [P, QB, D], F32, two)
        y16 = [sb(f"y16_{p}", [P, 2, KD, QB * S], F16, two) for p in range(2)]
        hid = [sb(f"hid{p}", [P, QB * S], F32, two) for p in range(HBUF)]
        hidl = [sb(f"hidl{p}", [P, QB * S], F16, two) for p in range(HBUF)]
        ystage = [sb(f"ystage{p}", [P, QB, D], F32, two) for p in range(2)]
        two.close()

        bank = [top.enter_context(nc.psum_tensor(f"bank{i}", [P, 512], F32)) for i in range(8)]
        tr_bank, pj_bank = bank[0], bank[1]
        sm_bank, st_bank, pv_bank = bank[2:4], bank[4:6], bank[6:8]
        yt_bank, h_bank = bank[0:2], bank[2:4]
        y_bank = [bank[4:6], bank[6:8]]

        consts_set, k_rows_set = sem("consts_set"), sem("k_rows_set")
        weights_in = sem("weights_in")
        patterns_set = sem("patterns_set")
        mask_in = sem("mask_in")
        mask_f32 = sem("mask_f32")
        mask_transposed = sem("mask_transposed")
        mask_copied = sem("mask_copied")
        mask_counted = sem("mask_counted")
        mask_set = sem("mask_set")
        masks_picked, v_masked = sem("masks_picked"), sem("v_masked")
        gates_in = sem("gates_in")
        gates_set = sem("gates_set")
        x_in = [sem(f"x_in{p}") for p in range(2)]
        ctx_loaded = [sem(f"ctx_loaded{p}") for p in range(2)]
        ln_step = sem("ln_step")
        ln_ready, ln_done = sem("ln_ready"), sem("ln_done")
        x_transposed, xT_copied = sem("x_transposed"), sem("xT_copied")
        ctx_transposed, ctxT_copied = sem("ctx_transposed"), sem("ctxT_copied")
        q_made, q_high, q_split = sem("q_made"), sem("q_high"), sem("q_split")
        k_made, k_high, k_split = sem("k_made"), sem("k_high"), sem("k_split")
        v_made, v_high, v_split = sem("v_made"), sem("v_high"), sem("v_split")
        q_moved = [sem(f"q_moved{b}") for b in range(2)]
        k_moved = [sem(f"k_moved{b}") for b in range(2)]
        weights_permuted = sem("weights_permuted")
        rough_scored, max_taken = sem("rough_scored"), sem("max_taken")
        max_rounded, max_split = sem("max_rounded"), sem("max_split")
        max_transposed, maxT_copied = sem("max_transposed"), sem("maxT_copied")
        max_moved = [sem(f"max_moved{b}") for b in range(2)]
        scored, exp_done, prob_split = sem("scored"), sem("exp_done"), sem("prob_split")
        weighed, norm_read, norm_done = sem("weighed"), sem("norm_read"), sem("norm_done")
        attn_transposed, attnT_copied = sem("attn_transposed"), sem("attnT_copied")
        projected, x1_done = sem("projected"), sem("x1_done")

        ffn_in, b1_in, ffn_b2_in = sem("ffn_in"), sem("b1_in"), sem("ffn_b2_in")
        w_step, w_summed, w_ternary = sem("w_step"), sem("w_summed"), sem("w_ternary")
        w_transposed, wT_copied = sem("w_transposed"), sem("wT_copied")
        b2_scaled = sem("b2_scaled")
        y_step, y_ready, y_done = sem("y_step"), sem("y_ready"), sem("y_done")
        y_transposed, y_high, y_split = sem("y_transposed"), sem("y_high"), sem("y_split")
        biased = sem("biased")
        h_made, gelu_done, h_split = sem("h_made"), sem("gelu_done"), sem("h_split")
        h_used, y_added = sem("h_used"), sem("y_added")
        y_out = [sem(f"y_out{p}") for p in range(2)]

        NC_SETS = 3
        def move_parts(sp, g, b, parts, src, dst, moved):
            for i, part in enumerate(parts):
                sp.dma_start(dst[g.parity][i * HD:(i + 1) * HD, b], src[:, part, b]).then_inc(moved[b], 16)

        def move_heads(sp, g, b, split, free):
            if free is not None:
                sp.wait_ge(scored, free)
            sp.wait_ge(q_split, split)
            move_parts(sp, g, b, (0, 1, 0), q16[g.parity], q_rows, q_moved)
            sp.wait_ge(k_split, split)
            move_parts(sp, g, b, (0, 0, 1), k16, k_rows, k_moved)

        def move_max(sp, g, b, copied):
            sp.wait_ge(maxT_copied, copied)
            sp.dma_start(q_rows[g.parity][HR:SR, b], smaxT[b][:]).then_inc(max_moved[b], 16)

        def load_x(sp, g):
            sp.dma_start(xres[:, bass.ds(g.batch(0), 2), :], x_v[:, bass.ds(g.batch(0), 2), :]).then_inc(
                x_in[g.parity], 16)

        def load_ctx(sp, g):
            sp.dma_start(ctx_sb[g.parity][:], ctx_v[:, bass.ds(g.batch(0), 2), :]).then_inc(
                ctx_loaded[g.parity], 16)

        def sp_group(sp, g, left):
            first = isinstance(g.half, int) and g.n == 0

            def held(value):
                return value if isinstance(value, int) else sp.snap(value)

            split1, split2 = held(g.n + 2), held(g.n + 3)
            scored_before = None if first else held(2 * UNITS * g.n)
            scored_b0 = held(2 * UNITS * g.n + UNITS)
            max_b1, max_b0 = held(g.batch(1) + 1), held(g.batch(0) + 3)
            x_past = held(2 * (g.n + 3))
            if left >= 4:
                sp.wait_ge(ln_done, x_past)
                load_x(sp, g.after(4))
            if left >= 3:
                sp.wait_ge(ctx_transposed, split1)
                load_ctx(sp, g.after(3))
            if left >= 1:
                move_heads(sp, g.after(1), 1, split1, scored_before)
            move_max(sp, g, 1, max_b1)
            if left >= 2:
                move_heads(sp, g.after(2), 0, split2, scored_b0)
            if left >= 1:
                move_max(sp, g.after(1), 0, max_b0)

        def transpose_x(pe, g, tr_free):
            for busy in tr_free:
                pe.wait_ge(*busy)
            pe.wait_ge(ln_done, 2 * (g.n + 1))
            for k in range(KD):
                for b in range(2):
                    last = pe.transpose(tr_bank[:, k * T + b * S:k * T + (b + 1) * S],
                                        xln[:, b, k * P:(k + 1) * P], ident[:])
            last.then_inc(x_transposed, 1)
            return [(xT_copied, g.n + 1)]

        def transpose_ctx(pe, g, tr_free):
            for busy in tr_free:
                pe.wait_ge(*busy)
            pe.wait_ge(ctx_loaded[g.parity], 16 * (g.half + 1))
            for b in range(2):
                pe.transpose(tr_bank[:, b * S:(b + 1) * S], ctx_sb[g.parity][:, b, 0:P], ident[:])
            for b in range(2):
                last = pe.transpose(tr_bank[0:C1, T + b * S:T + (b + 1) * S],
                                    ctx_sb[g.parity][:, b, P:C], ident[:])
            last.then_inc(ctx_transposed, 1)
            return [(ctxT_copied, g.n + 1)]

        def project_q(pe, g, m):
            if m == 0:
                pe.wait_ge(xT_copied, g.n + 1)
            for k in range(KD):
                last = pe.matmul(pj_bank[:, m * T:(m + 1) * T], wq_sb[:, k, m * P:(m + 1) * P],
                                 xlnT[:, k, :], start=(k == 0), stop=(k == KD - 1))
            if m == KD - 1:
                last.then_inc(q_made, 1)

        def project_k(pe, g, m):
            if m == 0:
                pe.wait_ge(ctxT_copied, g.n + 1)
            for k, rows in enumerate((P, C1)):
                last = pe.matmul(pj_bank[:, m * T:(m + 1) * T], wk_sb[0:rows, k, m * P:(m + 1) * P],
                                 ctxT[g.parity][0:rows, k, :], start=(k == 0), stop=(k == 1))
            if m == KD - 1:
                last.then_inc(k_made, 1)

        def project_v(pe, g, b):
            for k, rows in enumerate((P, C1)):
                last = pe.matmul(pj_bank[:, b * D:(b + 1) * D], ctxT[g.parity][0:rows, k, b * S:(b + 1) * S],
                                 wv_sb[0:rows, k, :], start=(k == 0), stop=(k == 1))
            if b == 1:
                last.then_inc(v_made, 1)

        def rough_scores(pe, g, b, u):
            n = g.batch(b) * UNITS + u
            if not (isinstance(n, int) and n < 2):
                pe.wait_ge(max_taken, n - 1)
            if u == 0:
                pe.wait_ge(k_moved[b], 16 * 3 * (g.n + 1))
                pe.wait_ge(q_moved[b], 16 * 3 * (g.n + 1))
            for c in range(UH):
                last = pe.matmul(sm_bank[u % 2][:, c * S:(c + 1) * S],
                                 q_rows[g.parity][0:HD, b, u * UH + c, :],
                                 k_rows[g.parity][0:HD, b, u * UH + c, :], start=True, stop=True)
            last.then_inc(rough_scored, 1)

        def transpose_max(pe, g, b, tr_free):
            for busy in tr_free:
                pe.wait_ge(*busy)
            n = g.batch(b)
            pe.wait_ge(max_split, n + 1)
            pe.transpose(tr_bank[0:2 * HEADS, 0:S // 2].bitcast(F16), smax16[:, b, :],
                         ident16[:]).then_inc(max_transposed, 1)
            return [(maxT_copied, n + 1)]

        def scores(pe, g, b, u):
            n = g.batch(b) * UNITS + u
            if u == 0:
                pe.wait_ge(max_moved[b], 16 * (g.n + 1))
            if not (isinstance(n, int) and n < 2):
                pe.wait_ge(exp_done, n - 1)
            for c in range(UH):
                last = pe.matmul(st_bank[u % 2][:, c * S:(c + 1) * S],
                                 k_rows[g.parity][0:SR, b, u * UH + c, :],
                                 q_rows[g.parity][0:SR, b, u * UH + c, :], start=True, stop=True)
            last.then_inc(scored, 1)

        def weigh(pe, g, b, u):
            n = g.batch(b)
            half, c0 = u // 2, u % 2 * UH
            pe.wait_ge(prob_split, n * UNITS + (u + 1))
            if b == 0 and u == 0:
                pe.wait_ge(v_masked, g.n + 1)
                pe.wait_ge(v_split, g.n + 1)
            if u % 2 == 0 and not (isinstance(n, int) and n == 0):
                pe.wait_ge(norm_read, n * 2 + (half - 1))
            for c in range(UH):
                o = pv_bank[half][:, (c0 + c) * VC:(c0 + c + 1) * VC]
                v = v16[g.parity][:, b, u * UH + c, :]
                high = prob[u][:].bitcast(BF16)[:, 2 * c * S + 1:2 * (c + 1) * S:2]
                pe.matmul(o, high, v, start=True, stop=False)
                last = pe.matmul(o, probl[u][:, c * S:(c + 1) * S], v, start=False, stop=True)
            last.then_inc(weighed, 1)

        def transpose_attn(pe, n, b, tr_free):
            for busy in tr_free:
                pe.wait_ge(*busy)
            pe.wait_ge(norm_done, 2 * n + 2)
            for k in range(KD):
                last = pe.transpose(tr_bank[:, k * S:(k + 1) * S],
                                    attn[b][:].rearrange("p h d -> p (h d)")[:, k * P:(k + 1) * P], ident[:])
            last.then_inc(attn_transposed, 1)
            return [(attnT_copied, n + 1)]

        def project_out(pe, n, tr_free):
            for busy in tr_free:
                pe.wait_ge(*busy)
            pe.wait_ge(attnT_copied, n + 1)
            for k in range(KD):
                last = pe.matmul(tr_bank[:, 0:D], attnT[:, k, :], wo_sb[:, k, :], start=(k == 0),
                                 stop=(k == KD - 1))
            last.then_inc(projected, 1)
            return [(x1_done, n + 1)]

        def pe_first(pe):
            pe.wait_ge(consts_set, NC_SETS)
            pe.wait_ge(mask_f32, 1)
            pe.transpose(st_bank[0][:, 0:B], maskT, ident[:]).then_inc(mask_transposed, 1)
            pe.wait_ge(mask_copied, 1)
            pe.matmul(st_bank[1][:, 0:B], ones[:], vmask[:], start=True, stop=True).then_inc(mask_counted, 1)
            g0, g1 = Group(0, 0), Group(0, 1)
            pe.wait_ge(ln_done, 2)
            tr = transpose_x(pe, g0, [])
            pe.wait_ge(weights_in, 16 * 6)
            pe.wait_ge(weights_permuted, 4)
            for m in range(KD):
                project_q(pe, g0, m)
            tr = transpose_ctx(pe, g0, tr)
            pe.wait_ge(q_split, 1)
            for m in range(KD):
                project_k(pe, g0, m)
            tr = transpose_x(pe, g1, tr)
            pe.wait_ge(k_split, 1)
            for b in range(2):
                project_v(pe, g0, b)
            tr = transpose_ctx(pe, g1, tr)
            pe.wait_ge(v_split, 1)
            for m in range(KD):
                project_q(pe, g1, m)
            tr = transpose_x(pe, g0.after(2), tr)
            for u in range(2):
                rough_scores(pe, g0, 0, u)
            pe.wait_ge(q_split, 2)
            project_k(pe, g1, 0)
            for u in range(2, UNITS):
                rough_scores(pe, g0, 0, u)
            project_k(pe, g1, 1)
            transpose_max(pe, g0, 0, tr)
            for u in range(2):
                rough_scores(pe, g0, 1, u)

        def pe_group(pe, g, left):
            first = isinstance(g.half, int) and g.n == 0
            before, g1, g2 = g.after(-1), g.after(1), g.after(2)
            tr = [(maxT_copied, 1)] if first else []

            rough_scores(pe, g, 1, 2)
            scores(pe, g, 0, 0)
            if not first:
                weigh(pe, before, 1, 2)
                tr = project_out(pe, g.batch(0) - 2, tr)

            rough_scores(pe, g, 1, 3)
            scores(pe, g, 0, 1)
            if not first:
                weigh(pe, before, 1, 3)
            if left >= 2:
                pe.wait_ge(v_split, g.n + 1)
                project_q(pe, g2, 0)
                tr = transpose_ctx(pe, g2, tr)
                project_q(pe, g2, 1)

            if left >= 1:
                rough_scores(pe, g1, 0, 0)
            scores(pe, g, 0, 2)
            weigh(pe, g, 0, 0)
            tr = transpose_max(pe, g, 1, tr)

            if left >= 1:
                rough_scores(pe, g1, 0, 1)
            scores(pe, g, 0, 3)
            weigh(pe, g, 0, 1)
            if not first:
                tr = transpose_attn(pe, g.batch(0) - 1, 1, tr)
            if left >= 2:
                pe.wait_ge(q_split, g.n + 3)
                project_k(pe, g2, 0)
                project_k(pe, g2, 1)

            if left >= 1:
                rough_scores(pe, g1, 0, 2)
            scores(pe, g, 1, 0)
            weigh(pe, g, 0, 2)
            if not first:
                tr = project_out(pe, g.batch(0) - 1, tr)

            if left >= 1:
                rough_scores(pe, g1, 0, 3)
            scores(pe, g, 1, 1)
            weigh(pe, g, 0, 3)
            if left >= 3:
                tr = transpose_x(pe, g.after(3), tr)

            if left >= 1:
                rough_scores(pe, g1, 1, 0)
            scores(pe, g, 1, 2)
            weigh(pe, g, 1, 0)
            if left >= 1:
                tr = transpose_max(pe, g1, 0, tr)
                if left >= 2:
                    pe.wait_ge(k_split, g.n + 3)
                else:
                    pe.wait_ge(v_split, g.n + 1)
                project_v(pe, g1, 0)

            if left >= 1:
                rough_scores(pe, g1, 1, 1)
            scores(pe, g, 1, 3)
            weigh(pe, g, 1, 1)
            tr = transpose_attn(pe, g.batch(0), 0, tr)
            if left >= 1:
                project_v(pe, g1, 1)

            if left == 0:
                tr = project_out(pe, g.batch(0), tr)
                for u in range(2, UNITS):
                    weigh(pe, g, 1, u)
                tr = transpose_attn(pe, g.batch(1), 1, tr)
                project_out(pe, g.batch(1), tr)

        def apply_x(act, g):
            act.wait_ge(ln_ready, g.n + 1)
            if not (isinstance(g.half, int) and g.n == 0):
                act.wait_ge(x_transposed, g.n)
            for b in range(2):
                act.activation(xln[:, b, :], row_of(g.batch(b)), ACT.Identity, bias=rstd[:, 3, b:b + 1],
                               scale=rstd[:, 1, b:b + 1]).then_inc(ln_done, 1)

        def copy_xT(act, g):
            act.wait_ge(x_transposed, g.n + 1)
            if not (isinstance(g.half, int) and g.n == 0):
                act.wait_ge(q_made, g.n)
            act.copy(xlnT[:].rearrange("p k t -> p (k t)"), tr_bank[:]).then_inc(xT_copied, 1)

        def copy_ctxT(act, g):
            act.wait_ge(ctx_transposed, g.n + 1)
            if not (isinstance(g.half, int) and g.n < 2):
                act.wait_ge(v_made, g.n - 1)
            act.copy(ctxT[g.parity][:, 0, :], tr_bank[:, 0:T])
            act.copy(ctxT[g.parity][0:C1, 1, :], tr_bank[0:C1, T:2 * T]).then_inc(ctxT_copied, 1)

        def by_batch(psum):
            return psum[:].rearrange("p (m b s) -> p b m s", m=KD, b=2)

        def high_q(act, g):
            act.wait_ge(q_made, g.n + 1)
            if not (isinstance(g.half, int) and g.n < 2):
                for b in range(2):
                    act.wait_ge(q_moved[b], 16 * 3 * (g.n - 1))
            act.copy(q16[g.parity][:, 0], by_batch(pj_bank)).then_inc(q_high, 1)

        def high_k(act, g):
            act.wait_ge(k_made, g.n + 1)
            if not (isinstance(g.half, int) and g.n == 0):
                for b in range(2):
                    act.wait_ge(k_moved[b], 16 * 3 * g.n)
            act.copy(k16[:, 0], by_batch(pj_bank)).then_inc(k_high, 1)

        def high_v(act, g):
            act.wait_ge(v_made, g.n + 1)
            if not (isinstance(g.half, int) and g.n < 2):
                act.wait_ge(weighed, 2 * UNITS * (g.n - 1))
            act.wait_ge(masks_picked, g.n + 1)
            for b in range(2):
                last = act.activation(v16[g.parity][:, b, :, 0:HD],
                                      pj_bank[:, b * D:(b + 1) * D].rearrange("p (h d) -> p h d", h=HEADS),
                                      ACT.Identity, bias=0.0, scale=masks[g.parity][:, b:b + 1])
            last.then_inc(v_high, 1)

        def copy_maxT(act, g, b):
            n = g.batch(b)
            act.wait_ge(max_transposed, n + 1)
            if not (isinstance(g.half, int) and g.n == 0):
                act.wait_ge(max_moved[b], 16 * g.n)
            act.copy(smaxT[b][:],
                     tr_bank[0:2 * HEADS, 0:S // 2].bitcast(F16)).then_inc(maxT_copied, 1)

        def exponentials(act, g, b, u):
            n = g.batch(b) * UNITS + u
            act.wait_ge(scored, n + 1)
            if not (isinstance(n, int) and n < UNITS):
                act.wait_ge(weighed, n - (UNITS - 1))
            act.activation(prob[u][:], st_bank[u % 2][:], ACT.Exp, bias=0.0,
                           scale=masks[g.parity][:, 2 + b:3 + b]).then_inc(exp_done, 1)

        def copy_attnT(act, n):
            act.wait_ge(attn_transposed, n + 1)
            if not (isinstance(n, int) and n == 0):
                act.wait_ge(projected, n)
            act.copy(attnT[:].rearrange("p k t -> p (k t)"), tr_bank[:, 0:KD * S]).then_inc(attnT_copied, 1)

        def act_first(act):
            g0, g1 = Group(0, 0), Group(0, 1)
            apply_x(act, g0)
            act.wait_ge(gates_in, 32)
            act.activation(gates[:, 2:4], gates[:, 0:2], ACT.Tanh).then_inc(gates_set, 1)
            copy_xT(act, g0)
            high_q(act, g0)
            copy_ctxT(act, g0)
            apply_x(act, g1)
            high_k(act, g0)
            copy_xT(act, g1)
            high_v(act, g0)
            copy_ctxT(act, g1)
            apply_x(act, g0.after(2))
            high_q(act, g1)
            copy_xT(act, g0.after(2))
            copy_maxT(act, g0, 0)
            high_k(act, g1)

        def act_group(act, g, left):
            first = isinstance(g.half, int) and g.n == 0
            g1, g2, g3 = g.after(1), g.after(2), g.after(3)
            exponentials(act, g, 0, 0)
            exponentials(act, g, 0, 1)
            if left >= 2:
                copy_ctxT(act, g2)
                high_q(act, g2)
            copy_maxT(act, g, 1)
            exponentials(act, g, 0, 2)
            exponentials(act, g, 0, 3)
            if not first:
                copy_attnT(act, g.batch(0) - 1)
            if left >= 3:
                apply_x(act, g3)
            if left >= 2:
                high_k(act, g2)
            exponentials(act, g, 1, 0)
            exponentials(act, g, 1, 1)
            if left >= 3:
                copy_xT(act, g3)
            exponentials(act, g, 1, 2)
            if left >= 1:
                copy_maxT(act, g1, 0)
            exponentials(act, g, 1, 3)
            copy_attnT(act, g.batch(0))
            if left >= 1:
                high_v(act, g1)
            if left == 0:
                copy_attnT(act, g.batch(1))

        def ln_part(dve, i, rows, step, base, ready):
            n = len(rows)
            half, y, t, shift = (rstd[:, k, 0:n] for k in range(4))
            if i > 0:
                dve.wait_ge(step, base + i)
            if i == 0:
                for b, row in enumerate(rows):
                    last = dve.bn_stats(stats[:, b, :], row)
            elif i == 1:
                dve.tensor_copy(t, stats[:, 0:n, 1])
                for b in range(n):
                    last = dve.bn_aggr(meanvar[:, b, :], stats[:, b, :])
            elif i == 2:
                last = dve.tensor_scalar(t, meanvar[:, 0:n, 1], EPS, None, ALU.add)
            elif i == 3:
                dve.tensor_scalar(y.bitcast(I32), t.bitcast(I32), -0.5, RSQRT_SEED, ALU.mult, ALU.add)
                last = dve.tensor_scalar(half, t, -0.5, None, ALU.mult)
            elif i == LN_PARTS - 1:
                dve.scalar_tensor_tensor(shift, meanvar[:, 0:n, 0], -1.0, y, ALU.mult,
                                         ALU.mult).then_inc(ready, 1)
                return
            elif i % 3 == 1:
                last = dve.tensor_tensor(t, y, y, ALU.mult)
            elif i % 3 == 2:
                last = dve.tensor_tensor(t, t, half, ALU.mult)
            else:
                last = dve.scalar_tensor_tensor(y, t, 1.5, y, ALU.add, ALU.mult)
            last.then_inc(step, 1)

        def row_of(batch):
            return xres[:, bass.ds(batch, 1), :].rearrange("p o d -> p (o d)")

        def norm_x(dve, g, parts):
            for i in parts:
                if i == 0:
                    dve.wait_ge(x_in[g.parity], 16 * (g.half + 1))
                if i == 3 and not (isinstance(g.half, int) and g.n == 0):
                    dve.wait_ge(ln_done, 2 * g.n)
                rows = [row_of(g.batch(b)) for b in range(2)] if i == 0 else (None,) * 2
                ln_part(dve, i, rows, ln_step, g.n * (LN_PARTS - 1), ln_ready)

        def low_q(dve, g):
            dve.wait_ge(q_high, g.n + 1)
            for b in range(2):
                last = dve.tensor_tensor(q16[g.parity][:, 1, b], by_batch(pj_bank)[:, b], q16[g.parity][:, 0, b],
                                         ALU.subtract)
            last.then_inc(q_split, 1)

        def low_k(dve, g):
            dve.wait_ge(k_high, g.n + 1)
            for b in range(2):
                last = dve.tensor_tensor(k16[:, 1, b], by_batch(pj_bank)[:, b], k16[:, 0, b], ALU.subtract)
            last.then_inc(k_split, 1)

        def pick_masks(pool, g):
            if not (isinstance(g.half, int) and g.n < 2):
                pool.wait_ge(weighed, 2 * UNITS * (g.n - 1))
            for c, source in ((0, vmask), (2, escale)):
                last = pool.tensor_tensor(masks[g.parity][:, c:c + 2], source[:, bass.ds(g.batch(0), 2)],
                                          ones[:, 0:2], ALU.mult)
            last.then_inc(masks_picked, 1)
            pool.wait_ge(masks_picked, g.n + 1)
            for b in range(2):
                last = pool.tensor_tensor(v16[g.parity][:, b, :, 2 * HD], ones[:, 0:HEADS],
                                          masks[g.parity][:, b:b + 1].to_broadcast([P, HEADS]), ALU.mult)
            last.then_inc(v_masked, 1)

        def low_v(dve, g):
            dve.wait_ge(v_high, g.n + 1)
            for b in range(2):
                last = dve.scalar_tensor_tensor(
                    v16[g.parity][:, b, :, HD:2 * HD],
                    pj_bank[:, b * D:(b + 1) * D].rearrange("p (h d) -> p h d", h=HEADS),
                    masks[g.parity][:, b:b + 1], v16[g.parity][:, b, :, 0:HD], ALU.mult, ALU.subtract)
            last.then_inc(v_split, 1)

        def take_max(dve, g, b, u):
            n = g.batch(b) * UNITS + u
            dve.wait_ge(rough_scored, n + 1)
            dve.tensor_reduce(smax[:, b, u * UH:(u + 1) * UH],
                              sm_bank[u % 2][:].rearrange("p (h j) -> p h j", h=UH), AX.X,
                              ALU.max).then_inc(max_taken, 1)

        def round_max(dve, g, b):
            n = g.batch(b)
            dve.wait_ge(max_taken, (n + 1) * UNITS)
            dve.tensor_scalar(smax16[:, b, 0:HEADS], smax[:, b, :], 1.0 / MAX_UNIT, None,
                              ALU.mult).then_inc(max_rounded, 1)

        def low_max(dve, g, b):
            n = g.batch(b)
            dve.wait_ge(max_rounded, n + 1)
            dve.scalar_tensor_tensor(smax16[:, b, HEADS:2 * HEADS], smax[:, b, :], 1.0 / MAX_UNIT,
                                     smax16[:, b, 0:HEADS], ALU.mult, ALU.subtract).then_inc(max_split, 1)

        HB = HEADS // 2

        def read_weighed(dve, n, b, half):
            heads = slice(half * HB, (half + 1) * HB)
            dve.wait_ge(weighed, n * UNITS + 2 * (half + 1))
            if not (isinstance(n, int) and n < 2):
                dve.wait_ge(attn_transposed, n - 1)
            pv = pv_bank[half][:, 0:HB * VC].rearrange("p (h c) -> p h c", h=HB)
            dve.reciprocal(rsum[:, b, heads], pv[:, :, 2 * HD])
            dve.tensor_reduce(attn[b][:, heads, :],
                              pv[:, :, 0:2 * HD].rearrange("p h (two d) -> p h d two", two=2), AX.X,
                              ALU.add).then_inc(norm_read, 1)

        def normalise(dve, n, b, half):
            heads = slice(half * HB, (half + 1) * HB)
            dve.wait_ge(norm_read, n * 2 + (half + 1))
            dve.tensor_tensor(attn[b][:, heads, :], attn[b][:, heads, :],
                              rsum[:, b, heads].unsqueeze(2).to_broadcast([P, HB, HD]),
                              ALU.mult).then_inc(norm_done, 1)

        def add_attention(dve, n):
            dve.wait_ge(projected, n + 1)
            row = xres[:, bass.ds(n, 1), :].rearrange("p o d -> p (o d)")
            dve.scalar_tensor_tensor(row, tr_bank[:, 0:D], gate_x, row, ALU.mult, ALU.add).then_inc(x1_done, 1)

        def dve_first(dve):
            dve.memset(ones[:], 1.0).then_inc(consts_set, 1)
            dve.wait_ge(mask_in, 16)
            dve.tensor_copy(maskT, escale[:].bitcast(U8)[:, 0:B]).then_inc(mask_f32, 1)
            g0, g1 = Group(0, 0), Group(0, 1)
            norm_x(dve, g0, range(LN_PARTS))
            dve.wait_ge(mask_transposed, 1)
            dve.tensor_copy(vmask[:], st_bank[0][:, 0:B]).then_inc(mask_copied, 1)
            dve.wait_ge(weights_in, 16 * 6)
            for raw, w in ((wq_raw, wq_sb), (wk_raw, wk_sb)):
                for k in range(2):
                    rows = C1 if raw is wk_raw and k == 1 else P
                    for m in range(KD):
                        last = dve.tensor_copy(
                            w[0:rows, k, m * P:(m + 1) * P].rearrange("p (d j) -> p d j", d=HD),
                            raw[0:rows, k, :].rearrange("p (j m d) -> p m d j", m=KD, d=HD)[:, m])
                    last.then_inc(weights_permuted, 1)
            dve.wait_ge(mask_counted, 1)
            dve.tensor_scalar(maskT, st_bank[1][:, 0:B], 0.5, None, ALU.is_lt)
            dve.tensor_scalar(escale[:], st_bank[1][:, 0:B], 0.5, SCALE, ALU.is_gt, ALU.mult).then_inc(mask_f32, 1)
            dve.wait_ge(mask_f32, 2)
            dve.tensor_tensor(vmask[:], vmask[:], maskT, ALU.max).then_inc(mask_set, 1)
            dve.wait_ge(mask_set, 1)
            norm_x(dve, g1, range(LN_PARTS))
            low_q(dve, g0)
            dve.wait_ge(gates_set, 1)
            low_k(dve, g0)
            norm_x(dve, g0.after(2), range(0, LN_AHEAD))
            low_v(dve, g0)
            norm_x(dve, g0.after(2), range(LN_AHEAD, LN_PARTS))
            low_q(dve, g1)
            for u in range(UNITS):
                take_max(dve, g0, 0, u)
            round_max(dve, g0, 0)
            low_max(dve, g0, 0)
            low_k(dve, g1)
            for u in range(2):
                take_max(dve, g0, 1, u)
            norm_x(dve, g0.after(3), range(0, LN_AHEAD))

        def dve_group(dve, g, left):
            first = isinstance(g.half, int) and g.n == 0
            g1, g2, g3, g4 = (g.after(k) for k in range(1, 5))

            def norm(i):
                if left == 0:
                    norm_y(dve, Group(0, 0), ((i - LN_AHEAD) % LN_PARTS,))
                if i < LN_AHEAD and left >= 4:
                    norm_x(dve, g4, (i,))
                if i >= LN_AHEAD and left >= 3:
                    norm_x(dve, g3, (i,))

            take_max(dve, g, 1, 2)
            norm(8)
            if not first:
                add_attention(dve, g.batch(0) - 2)
            norm(9)
            take_max(dve, g, 1, 3)
            round_max(dve, g, 1)
            norm(10)
            low_max(dve, g, 1)
            if not first:
                read_weighed(dve, g.batch(0) - 1, 1, 1)
                normalise(dve, g.batch(0) - 1, 1, 1)
            norm(11)
            if left >= 2:
                low_q(dve, g2)
            norm(12)
            if left >= 1:
                take_max(dve, g1, 0, 0)
            norm(13)
            if left >= 1:
                take_max(dve, g1, 0, 1)
            read_weighed(dve, g.batch(0), 0, 0)
            normalise(dve, g.batch(0), 0, 0)
            if left >= 1:
                take_max(dve, g1, 0, 2)
            if left >= 2:
                low_k(dve, g2)
            if not first:
                add_attention(dve, g.batch(0) - 1)
            if left >= 1:
                take_max(dve, g1, 0, 3)
                round_max(dve, g1, 0)
                low_max(dve, g1, 0)
            norm(0)
            read_weighed(dve, g.batch(0), 0, 1)
            norm(1)
            normalise(dve, g.batch(0), 0, 1)
            norm(2)
            if left >= 1:
                take_max(dve, g1, 1, 0)
            norm(3)
            if left >= 1:
                take_max(dve, g1, 1, 1)
            norm(4)
            read_weighed(dve, g.batch(1), 1, 0)
            norm(5)
            normalise(dve, g.batch(1), 1, 0)
            norm(6)
            if left >= 1:
                low_v(dve, g1)
            norm(7)
            if left == 0:
                sum_weights(dve, 0)
                add_attention(dve, g.batch(0))
                read_weighed(dve, g.batch(1), 1, 1)
                normalise(dve, g.batch(1), 1, 1)
                sum_weights(dve, 1)
                add_attention(dve, g.batch(1))

        def low_prob(pool, g, b, u):
            n = g.batch(b) * UNITS + u
            pool.wait_ge(exp_done, n + 1)
            pool.tensor_tensor(probl[u][:], prob[u][:], prob[u][:].bitcast(BF16)[:, 1::2],
                               ALU.subtract).then_inc(prob_split, 1)

        def pool_group(pool, g, left):
            for b in range(2):
                for u in range(UNITS):
                    low_prob(pool, g, b, u)
                    if b == 1 and u == 0 and left >= 1:
                        pick_masks(pool, g.after(1))

        def over_pairs(engine, do, pairs, apart=1):
            for s in range(2):
                do(engine, Group(0, s), 2 * pairs - 1 - s)
            with engine.Fori(1, pairs - apart) as i:
                for s in range(2):
                    do(engine, Group(i, s), 2 * apart + 1 - s)
            for r in range(pairs - apart, pairs):
                for s in range(2):
                    do(engine, Group(r, s), 2 * (pairs - r) - 1 - s)

        def over_groups(engine, do, apart=1):
            over_pairs(engine, do, NG // 2, apart)

        def steps(engine, do):
            over_pairs(engine, do, NQ // 2)

        def sum_weights(dve, i):
            dve.wait_ge(ffn_in, 16 * 2)
            dve.tensor_reduce(wstat[:, i:i + 1], (w1_raw, w2_raw)[i][:].rearrange("p a b -> p (a b)"), AX.X,
                              ALU.add, apply_absolute_value=True).then_inc(w_step, 1)

        def thresholds(dve):
            dve.wait_ge(w_summed, 1)
            dve.tensor_scalar(wstat[:, 2:4], h_bank[0][:, 0:2], 0.5 / float(FF * D), 0.5e-8, ALU.mult,
                              ALU.max).then_inc(w_step, 1)
            dve.wait_ge(w_step, 3)
            dve.tensor_scalar(wstat[:, 4:6], wstat[:, 2:4], -1.0, None, ALU.mult).then_inc(w_step, 1)
            dve.wait_ge(w_step, 4)

        def make_ternary(dve, i):
            raw, tern = ((w1_raw, w1_t), (w2_raw, w2_t))[i]
            flat = raw[:].rearrange("p a b -> p (a b)")
            if i:
                dve.wait_ge(w_ternary, i)
            dve.tensor_scalar(w_neg[:], flat, wstat[:, 4 + i:5 + i], None, ALU.is_lt).then_inc(w_step, 1)
            dve.wait_ge(w_step, 5 + i)
            dve.scalar_tensor_tensor(tern[:].rearrange("p a b -> p (a b)"), flat, wstat[:, 2 + i:3 + i],
                                     w_neg[:], ALU.is_gt, ALU.subtract).then_inc(w_ternary, 1)

        def scale_b2(dve):
            dve.wait_ge(ffn_b2_in, 16)
            dve.tensor_scalar(b2g[:], b2_sb[:], gate_f, None, ALU.mult).then_inc(b2_scaled, 1)

        def prepare_weights_pe(pe):
            pe.wait_ge(w_step, 2)
            pe.matmul(h_bank[0][:, 0:2], ones[:], wstat[:, 0:2], start=True, stop=True).then_inc(w_summed, 1)
            transpose_y(pe, Group(0, 0))
            n = 0
            for i, (tern, rows, cols) in enumerate(((w1_t, FB, KD), (w2_t, KD, FB))):
                pe.wait_ge(w_ternary, i + 1)
                for c in range(cols):
                    for r in range(rows):
                        q, o = n // 8, n % 8
                        if o == 0 and q >= 2:
                            pe.wait_ge(wT_copied, q - 1)
                        last = pe.transpose(y_bank[0][q % 2][:].bitcast(F16)[:, o * P:(o + 1) * P],
                                            tern[:, r, c * P:(c + 1) * P], ident16[:])
                        n += 1
                        if o == 7:
                            last.then_inc(w_transposed, 1)
                if i == 0:
                    pe.wait_ge(wT_copied, 2)
                    for f in range(LAG):
                        hidden(pe, Group(0, 0), f)

        def prepare_weights_act(act):
            flat = [w1T[:, k, :] for k in range(KD)] + [
                w2T[:, 4 * q:4 * q + 4, :].rearrange("p f d -> p (f d)") for q in range(FB // 4)]
            for q, dst in enumerate(flat):
                act.wait_ge(w_transposed, q + 1)
                act.copy(dst, y_bank[0][q % 2][:].bitcast(F16)).then_inc(wT_copied, 1)
                if q == 1:
                    act.wait_ge(b1_in, 16)
                    for f in range(LAG):
                        gelu(act, Group(0, 0), f)

        def norm_y(dve, g, parts):
            for i in parts:
                if i == 3 and not (isinstance(g.half, int) and g.n == 0):
                    dve.wait_ge(y_done, QB * g.n)
                rows = [row_of(g.n * QB + b) for b in range(QB)] if i == 0 else (None,) * QB
                ln_part(dve, i, rows, y_step, g.n * (LN_PARTS - 1), y_ready)

        def apply_y(act, g, batches):
            act.wait_ge(y_ready, g.n + 1)
            if not (isinstance(g.half, int) and g.n == 0):
                act.wait_ge(y_transposed, KD * g.n)
            for b in batches:
                act.activation(yln[:, b, :], row_of(g.n * QB + b), ACT.Identity, bias=rstd[:, 3, b:b + 1],
                               scale=rstd[:, 1, b:b + 1]).then_inc(y_done, 1)

        def transpose_y(pe, g):
            pe.wait_ge(y_done, QB * (g.n + 1))
            for k in range(KD):
                if not (isinstance(g.half, int) and g.n == 0):
                    pe.wait_ge(y_split, KD * g.n)
                for b in range(QB):
                    last = pe.transpose(yt_bank[k][:, b * S:(b + 1) * S], yln[:, b, k * P:(k + 1) * P], ident[:])
                last.then_inc(y_transposed, 1)

        def high_y(act, g):
            for k in range(KD):
                act.wait_ge(y_transposed, KD * g.n + (k + 1))
                if k == 0 and not (isinstance(g.half, int) and g.n < 2):
                    act.wait_ge(h_made, FB * (g.n - 1))
                act.copy(y16[g.parity][:, 0, k, :], yt_bank[k][:]).then_inc(y_high, 1)

        def low_y(dve, g):
            for k in range(KD):
                dve.wait_ge(y_high, KD * g.n + (k + 1))
                dve.tensor_tensor(y16[g.parity][:, 1, k, :], yt_bank[k][:], y16[g.parity][:, 0, k, :],
                                  ALU.subtract).then_inc(y_split, 1)

        def hidden(pe, g, f):
            n = g.n * FB + f
            if f == 0:
                pe.wait_ge(y_split, KD * (g.n + 1))
            if not (isinstance(n, int) and n < 2):
                pe.wait_ge(gelu_done, n - 1)
            i = 0
            for k in range(KD):
                for part in range(2):
                    last = pe.matmul(h_bank[f % 2][:], w1T[:, k, f * P:(f + 1) * P], y16[g.parity][:, part, k, :],
                                     start=(i == 0), stop=(i == 2 * KD - 1))
                    i += 1
            last.then_inc(h_made, 1)

        def gelu(act, g, f):
            n = g.n * FB + f
            act.wait_ge(h_made, n + 1)
            if not (isinstance(n, int) and n < HBUF):
                act.wait_ge(h_used, n - (HBUF - 1))
            act.activation(hid[f % HBUF][:], h_bank[f % 2][:], ACT.Gelu, bias=b1_sb[:, f:f + 1]).then_inc(gelu_done, 1)

        def low_h(dve, g, f):
            n = g.n * FB + f
            dve.wait_ge(gelu_done, n + 1)
            dve.tensor_tensor(hidl[f % HBUF][:], hid[f % HBUF][:], hid[f % HBUF][:].bitcast(BF16)[:, 1::2],
                              ALU.subtract).then_inc(h_split, 1)

        def second(pe, g, f):
            n = g.n * FB + f
            if f == 0 and not (isinstance(g.half, int) and g.n < 2):
                pe.wait_ge(y_added, QB * (g.n - 1))
            pe.wait_ge(h_split, n + 1)
            for b in range(QB):
                o = y_bank[g.parity][b // 2][:, (b % 2) * D:(b % 2 + 1) * D]
                high = hid[f % HBUF][:].bitcast(BF16)[:, 2 * b * S + 1:2 * (b + 1) * S:2]
                pe.matmul(o, high, w2T[:, f, :], start=(f == 0 and b % 2 == 0), stop=False, skip_group_check=True)
                last = pe.matmul(o, hidl[f % HBUF][:, b * S:(b + 1) * S], w2T[:, f, :], start=False,
                                 stop=(f == FB - 1), skip_group_check=True)
            last.then_inc(h_used, 1)

        def pe_step(pe, g, left):
            first = isinstance(g.half, int) and g.n == 0
            for f in range(FB):
                if not (first and f < LAG):
                    hidden(pe, g, f)
                if first and f == LAG:
                    pe.wait_ge(wT_copied, 4)
                if f >= LAG:
                    second(pe, g, f - LAG)
                elif not first:
                    second(pe, g.after(-1), FB - LAG + f)
                if f == FB - 2 and left >= 1:
                    transpose_y(pe, g.after(1))
            if left == 0:
                for f in range(FB - LAG, FB):
                    second(pe, g, f)

        def act_step(act, g, left):
            first = isinstance(g.half, int) and g.n == 0
            for f in range(FB):
                if not (first and f < LAG):
                    gelu(act, g, f)
                if f in (4, 5) and left >= 1:
                    apply_y(act, g.after(1), range((f - 4) * QB // 2, (f - 3) * QB // 2))
                if f == FB - 2 and left >= 1:
                    high_y(act, g.after(1))

        def add_y(dve, g, batches):
            dve.wait_ge(h_used, FB * (g.n + 1))
            dve.wait_ge(biased, g.n + 1)
            if not (isinstance(g.half, int) and g.n < 2):
                dve.wait_ge(y_out[g.parity], 16 * g.half)
            for b in batches:
                o = y_bank[g.parity][b // 2][:, (b % 2) * D:(b % 2 + 1) * D]
                dve.scalar_tensor_tensor(ystage[g.parity][:, b, :], o, gate_f,
                                         xres[:, bass.ds(g.n * QB + b, 1), :].rearrange("p o d -> p (o d)"),
                                         ALU.mult, ALU.add).then_inc(y_added, 1)

        def dve_step(dve, g, left):
            first = isinstance(g.half, int) and g.n == 0
            for f in range(FB):
                low_h(dve, g, f)
                if f < 4 and left >= 1:
                    norm_y(dve, g.after(1), (range(0, 2), range(2, 6), range(6, 10), range(10, LN_PARTS))[f])
                if f in (4, 5) and not first:
                    add_y(dve, g.after(-1), range((f - 4) * QB // 2, (f - 3) * QB // 2))
                if f == FB - 2 and left >= 1:
                    low_y(dve, g.after(1))
            if left == 0:
                add_y(dve, g, range(QB))

        def pool_step(pool, g, left):
            pool.wait_ge(y_done, QB * (g.n + 1))
            rows = xres[:, bass.ds(g.n * QB, QB), :]
            pool.tensor_tensor(rows, rows, b2g[:].unsqueeze(1).to_broadcast([P, QB, D]), ALU.add).then_inc(biased, 1)

        def sp_step(sp, g, left):
            sp.wait_ge(y_added, QB * (g.n + 1))
            sp.dma_start(out_v[:, bass.ds(g.n * QB, QB), :], ystage[g.parity][:]).then_inc(y_out[g.parity], 16)

        block = top.enter_context(nc.Block())

        @block.sync
        def _(sp):
            sp.dma_start(escale[:].bitcast(U8)[:, 0:S], mask).then_inc(mask_in, 16)
            load_x(sp, Group(0, 0))
            load_ctx(sp, Group(0, 0))
            load_x(sp, Group(0, 1))
            sp.dma_start(wq_raw, wq.rearrange("(k p) n -> p k n", p=P)).then_inc(weights_in, 16)
            sp.dma_start(wk_raw[:, 0, :], wk[0:P, :]).then_inc(weights_in, 16)
            sp.dma_start(wk_raw[0:C1, 1, :], wk[P:C, :]).then_inc(weights_in, 16)
            sp.dma_start(wv_sb[:, 0, :], wv[0:P, :]).then_inc(weights_in, 16)
            sp.dma_start(wv_sb[0:C1, 1, :], wv[P:C, :]).then_inc(weights_in, 16)
            sp.dma_start(wo_sb[:], wo.rearrange("(k p) n -> p k n", p=P)).then_inc(weights_in, 16)
            load_ctx(sp, Group(0, 1))
            sp.dma_start(gates[:, 0:1], g_xattn.partition_broadcast(P)).then_inc(gates_in, 16)
            sp.dma_start(gates[:, 1:2], g_ffn.partition_broadcast(P)).then_inc(gates_in, 16)
            sp.wait_ge(ln_done, 2)
            load_x(sp, Group(1, 0))
            sp.wait_ge(ctx_transposed, 1)
            load_ctx(sp, Group(1, 0))
            sp.wait_ge(k_rows_set, 2)
            for b in range(2):
                move_heads(sp, Group(0, 0), b, 1, None)
            sp.wait_ge(ln_done, 4)
            load_x(sp, Group(1, 1))
            sp.wait_ge(rough_scored, 1)
            move_max(sp, Group(0, 0), 0, 1)
            move_heads(sp, Group(0, 1), 0, 2, None)
            over_groups(sp, sp_group, 2)
            sp.wait_ge(scored, 2 * UNITS * (NG - 1))
            sp.dma_start(w1_raw[:], w1.rearrange("(f p) d -> p f d", p=P)).then_inc(ffn_in, 16)
            sp.dma_start(w2_raw[:], w2.rearrange("(k p) f -> p k f", p=P)).then_inc(ffn_in, 16)
            sp.wait_ge(x1_done, B)
            with nc.allow_non_contiguous_dma(reason="1024 biases, one a row"):
                sp.dma_start(b1_sb[:], b1.rearrange("(f p) -> p f", p=P)).then_inc(b1_in, 16)
            sp.dma_start(b2_sb[:], b2.partition_broadcast(P)).then_inc(ffn_b2_in, 16)
            steps(sp, sp_step)
            for p in range(2):
                sp.wait_ge(y_out[p], 16 * (NQ // 2))

        @block.gpsimd
        def _(pool):
            pool.memset(ident[:], 0.0).then_inc(consts_set, 1)
            pool.wait_ge(consts_set, 2)
            pool.affine_select(out=ident[:], in_=ident[:], compare_op=ALU.not_equal, fill=1.0, base=0,
                               pattern=[[-1, P]], channel_multiplier=1).then_inc(patterns_set, 1)
            pool.wait_ge(patterns_set, 1)
            pool.tensor_copy(ident16[:], ident[:]).then_inc(consts_set, 1)
            pool.wait_ge(consts_set, NC_SETS)
            for p in range(2):
                if p:
                    pool.wait_ge(k_rows_set, p)
                pool.memset(k_rows[p][32:64].rearrange("p b h s -> p (b h s)"), -MAX_UNIT).then_inc(k_rows_set, 1)
            pool.wait_ge(k_rows_set, 2)
            pool.wait_ge(mask_set, 1)
            pick_masks(pool, Group(0, 0))
            over_groups(pool, pool_group)
            pool.wait_ge(b2_scaled, 1)
            steps(pool, pool_step)

        @block.tensor
        def _(pe):
            pe_first(pe)
            over_groups(pe, pe_group, 2)
            prepare_weights_pe(pe)
            steps(pe, pe_step)

        @block.scalar
        def _(act):
            act_first(act)
            over_groups(act, act_group, 2)
            act.wait_ge(x1_done, B)
            apply_y(act, Group(0, 0), range(QB))
            high_y(act, Group(0, 0))
            prepare_weights_act(act)
            steps(act, act_step)

        @block.vector
        def _(dve):
            dve_first(dve)
            over_groups(dve, dve_group, 2)
            dve.wait_ge(x1_done, B)
            thresholds(dve)
            make_ternary(dve, 0)
            low_y(dve, Group(0, 0))
            make_ternary(dve, 1)
            scale_b2(dve)
            steps(dve, dve_step)


_INS = ["x", "ctx_768", "mask_BxS2_bf1", "g_xattn", "g_ffn", "L0_xattn_Wq", "L0_xattn_Wk", "L0_xattn_Wv",
        "L0_xattn_Wo", "L0_ffn_W1", "L0_ffn_b1", "L0_ffn_W2", "L0_ffn_b2"]
_OUTS = [((128, 128, 256), "float32")]


def kernel(**inputs):
    import numpy as _np
    import concourse.bacc as _bacc
    from concourse import mybir as _mybir
    from concourse.bass_utils import run_bass_kernel_spmd as _run

    nc = _bacc.Bacc("TRN2", target_bir_lowering=False, num_devices=1)
    arrays, args = {}, []
    for name in _INS:
        a = _np.ascontiguousarray(inputs[name])
        arrays[f"in_{name}_dram"] = a
        args.append(nc.dram_tensor(f"in_{name}_dram", a.shape, _mybir.dt.from_np(a.dtype), kind="ExternalInput").ap())
    for i, (shape, dtype) in enumerate(_OUTS):
        dt = _mybir.dt.from_np(_np.dtype(dtype))
        args.append(nc.dram_tensor(f"out_{i}_dram", shape, dt, kind="ExternalOutput").ap())
    bass_gated_cross_attention_ternary_ffn(nc, *args)
    r = _run(nc, [arrays], core_ids=[0])
    got = tuple(r.results[0][f"out_{i}_dram"] for i in range(len(_OUTS)))
    return got[0]
```
